# Optimizing a Trainium2 kernel written in Bass

```python
import numpy as np
import jax
import jax.numpy as jnp

def _softmax(x, axis=-1):
    return jax.nn.softmax(x, axis=axis)

def _gelu(x):
    return jax.nn.gelu(x, approximate=True)

def _silu(x):
    return jax.nn.silu(x)

def _sigmoid(x):
    return jax.nn.sigmoid(x)

def _layernorm(x, axis=-1, eps=1e-05):
    m = jnp.mean(x, axis=axis, keepdims=True)
    v = jnp.var(x, axis=axis, keepdims=True)
    return (x - m) / jnp.sqrt(v + eps)

def _scatter_add(tgt, idx, src, axis=0):
    return tgt.at[idx].add(src)

def _segment_sum(src, seg, n):
    return jax.ops.segment_sum(src, seg, n)
kernel_name = 'mk_flamingo_gated_d1_seqx_r4_20d72e'

def setup_inputs(seed: int=0):
    np.random.seed(seed)
    _w = jnp.asarray

    def _rec_inputs():
        import jax
        import jax.numpy as jnp
        _rk = jax.random.key(seed)
        x = 7.22e-05 + 1 * jax.random.normal(jax.random.fold_in(_rk, 1), (8, 512, 256), jnp.float32)
        _lenS = 512 - jax.random.randint(jax.random.fold_in(_rk, 7), (8,), 0, max(1, 512 // 4) + 1, jnp.int32)
        _lenS2 = 64 - jax.random.randint(jax.random.fold_in(_rk, 8), (8,), 0, max(1, 64 // 4) + 1, jnp.int32)
        _ctx_1024P = jax.random.normal(jax.random.fold_in(_rk, 11), (8, 16, 256), jnp.float32)
        _ctx_1024c = jax.random.dirichlet(jax.random.fold_in(_rk, 511), 0.3 * jnp.ones((16,), jnp.float32), (8, 64))
        _ctx_1024t = jnp.einsum('bsk,bkd->bsd', _ctx_1024c, _ctx_1024P)
        _ctx_1024t = _ctx_1024t * jax.lax.rsqrt(jnp.mean(jnp.square(_ctx_1024t)) + 1e-12) * 0.953939
        ctx_1024 = 4.13588e-05 + 0.999923 * (_ctx_1024t + 0.3 * jax.random.normal(jax.random.fold_in(_rk, 611), (8, 64, 256), jnp.float32))
        _validS = jnp.arange(512)[None, :] < _lenS[:, None]
        _validS2 = jnp.arange(64)[None, :] < _lenS2[:, None]
        _causal = jnp.tril(jnp.ones((512, 512), dtype=bool))
        mask_Bx1xSxS2_if1 = jnp.where(jnp.ones((8, 1, 512, 64), dtype=bool), 1, 0).astype(jnp.int32)
        _g = jax.random.normal(jax.random.fold_in(_rk, 9001), (2, 1), jnp.float32)
        _g = jnp.sign(_g) * jnp.maximum(jnp.abs(_g), 1.0) + (_g == 0) * 1.0
        g_xattn = _g[0]
        g_ffn = _g[1]
        return (x, ctx_1024, mask_Bx1xSxS2_if1, g_xattn, g_ffn)
    x, ctx_1024, mask_Bx1xSxS2_if1, g_xattn, g_ffn = _rec_inputs()

    def _L0_xattn_setup():
        import jax, jax.numpy as jnp
        import numpy as np
        B, S, D = (4, 512, 256)
        H = 16
        DK = D // H

        def _split_heads(x):
            b, s, _ = x.shape
            return x.reshape(b, s, H, DK).transpose(0, 2, 1, 3)
        key = jax.random.key(seed)
        ks = jax.random.split(key, 8)
        scale = 1.0 / np.sqrt(D)
        return {'q': jax.random.normal(ks[0], (B, S, D), dtype=jnp.float32), 'k': jax.random.normal(ks[1], (B, S, D), dtype=jnp.float32), 'v': jax.random.normal(ks[2], (B, S, D), dtype=jnp.float32), 'mask': jnp.ones((B, 1, S, S), dtype=jnp.int32), 'Wq': jax.random.normal(ks[3], (D, D), dtype=jnp.float32) * scale, 'bq': jnp.zeros((D,), dtype=jnp.float32), 'Wo': jax.random.normal(ks[4], (D, D), dtype=jnp.float32) * scale, 'bo': jnp.zeros((D,), dtype=jnp.float32)}
    _L0_xattn_all = _L0_xattn_setup()
    _L0_xattn_in = {k: v for k, v in _L0_xattn_all.items() if k in ('Wq', 'bq', 'Wo', 'bo')}
    del _L0_xattn_all

    def _L0_ffn_setup():
        import jax, jax.numpy as jnp
        import numpy as np
        FEATURES = 256
        D_IN = 256

        def fp8_gemm_optimized(x, input_scale, kernel, kernel_scale):
            s_in = input_scale[0]
            s_k = kernel_scale[0]
            x_q = (x.astype(jnp.float32) / s_in).astype(jnp.float8_e4m3fn)
            k_q = (kernel.astype(jnp.float32) / s_k).astype(jnp.float8_e4m3fn)
            y = jnp.dot(x_q.astype(jnp.float32), k_q.astype(jnp.float32), preferred_element_type=jnp.float32)
            return y * (s_in * s_k)
        key = jax.random.key(seed)
        kx, kk, kb = jax.random.split(key, 3)
        x = jax.random.normal(kx, (4, 2048, D_IN), dtype=jnp.float32)
        limit = np.sqrt(6.0 / (D_IN + FEATURES)).astype(np.float32)
        kernel = jax.random.uniform(kk, (D_IN, FEATURES), dtype=jnp.float32, minval=-limit, maxval=limit).astype(jnp.bfloat16)
        input_scale = jnp.ones((1,), dtype=jnp.float32)
        kernel_scale = jnp.ones((1,), dtype=jnp.float32)
        bias = jnp.zeros((FEATURES,), dtype=jnp.bfloat16)
        return {'x': x, 'kernel': kernel, 'input_scale': input_scale, 'kernel_scale': kernel_scale, 'bias': bias}
    _L0_ffn_all = _L0_ffn_setup()
    _L0_ffn_in = {k: v for k, v in _L0_ffn_all.items() if k in ('kernel', 'input_scale', 'kernel_scale', 'bias')}
    del _L0_ffn_all
    return {'x': x, 'ctx_1024': ctx_1024, 'mask_Bx1xSxS2_if1': mask_Bx1xSxS2_if1, 'g_xattn': g_xattn, 'g_ffn': g_ffn, 'L0_xattn_Wq': _L0_xattn_in['Wq'], 'L0_xattn_bq': _L0_xattn_in['bq'], 'L0_xattn_Wo': _L0_xattn_in['Wo'], 'L0_xattn_bo': _L0_xattn_in['bo'], 'L0_ffn_kernel': _L0_ffn_in['kernel'], 'L0_ffn_input_scale': _L0_ffn_in['input_scale'], 'L0_ffn_kernel_scale': _L0_ffn_in['kernel_scale'], 'L0_ffn_bias': _L0_ffn_in['bias']}

def reference(x, ctx_1024, mask_Bx1xSxS2_if1, g_xattn, g_ffn, L0_xattn_Wq, L0_xattn_bq, L0_xattn_Wo, L0_xattn_bo, L0_ffn_kernel, L0_ffn_input_scale, L0_ffn_kernel_scale, L0_ffn_bias):
    import jax
    import jax.numpy as jnp

    def _L0_xattn_ref(q, k, v, mask, Wq, bq, Wo, bo):
        import jax, jax.numpy as jnp
        import numpy as np
        B, S, D = (4, 512, 256)
        H = 16
        DK = D // H

        def _split_heads(x):
            b, s, _ = x.shape
            return x.reshape(b, s, H, DK).transpose(0, 2, 1, 3)
        qh = _split_heads(q @ Wq.T + bq)
        kh = _split_heads(k @ Wq.T + bq)
        vh = _split_heads(v @ Wq.T + bq)
        scores = jnp.einsum('bhqd,bhkd->bhqk', qh, kh) / jnp.sqrt(jnp.float32(DK))
        scores = jnp.where(mask == 0, jnp.float32(-1000000000.0), scores)
        p_attn = jax.nn.softmax(scores, axis=-1)
        x = jnp.einsum('bhqk,bhkd->bhqd', p_attn, vh)
        x = x.transpose(0, 2, 1, 3).reshape(q.shape[0], -1, H * DK)
        return x @ Wo.T + bo

    def _L0_ffn_ref(x, kernel, input_scale, kernel_scale, bias):
        import jax, jax.numpy as jnp
        import numpy as np
        FEATURES = 256
        D_IN = 256

        def fp8_gemm_optimized(x, input_scale, kernel, kernel_scale):
            s_in = input_scale[0]
            s_k = kernel_scale[0]
            x_q = (x.astype(jnp.float32) / s_in).astype(jnp.float8_e4m3fn)
            k_q = (kernel.astype(jnp.float32) / s_k).astype(jnp.float8_e4m3fn)
            y = jnp.dot(x_q.astype(jnp.float32), k_q.astype(jnp.float32), preferred_element_type=jnp.float32)
            return y * (s_in * s_k)
        dtype = jnp.bfloat16
        x = x.astype(dtype)
        orig_shape = x.shape
        x2 = x.reshape(-1, x.shape[-1])
        y = fp8_gemm_optimized(x2, input_scale, kernel, kernel_scale)
        y = y.astype(dtype) + bias
        return y.reshape(orig_shape[:-1] + (FEATURES,))
    x = x + jnp.tanh(g_xattn[0]) * _L0_xattn_ref(_layernorm(x, axis=-1), ctx_1024, ctx_1024, mask_Bx1xSxS2_if1, L0_xattn_Wq, L0_xattn_bq, L0_xattn_Wo, L0_xattn_bo)
    x = x + jnp.tanh(g_ffn[0]) * _L0_ffn_ref(_layernorm(x, axis=-1), L0_ffn_kernel, L0_ffn_input_scale, L0_ffn_kernel_scale, L0_ffn_bias)
    return x

_drawn_inputs = setup_inputs


def setup_inputs(seed=0):
    import zlib

    import numpy as np

    out = dict(_drawn_inputs(seed))
    spreads = {'L0_xattn_bq': (0.0, 0.1), 'L0_xattn_bo': (0.0, 0.1), 'L0_ffn_bias': (0.0, 0.1)}
    factors = {}
    for name, (base, spread) in spreads.items():
        noise = np.random.default_rng([zlib.crc32(name.encode()), seed]).standard_normal(out[name].shape)
        drawn = base * np.exp(spread * noise) if base else spread * noise
        out[name] = jnp.asarray(drawn.astype(out[name].dtype))
    for name, factor in factors.items():
        out[name] = (out[name] * factor).astype(out[name].dtype)
    return out
```

```python
from contextlib import ExitStack

import numpy as np

import concourse.bass as bass
from concourse import mybir

ALU = mybir.AluOpType
ACT = mybir.ActivationFunctionType
AX_X = mybir.AxisListType.X
F32 = mybir.dt.float32
F32R = mybir.dt.float32r
BF16 = mybir.dt.bfloat16
FP8 = mybir.dt.float8e4
I32 = mybir.dt.int32

P = 128
MASKED = -(2.0 ** 100)
EPS = 1e-5
FP8_MAX = 240.0


def constants(D, H, KEYS):
    DK = D // H
    row = np.arange(P)
    pairs = H // 2
    ident = np.eye(P, dtype=np.float32)
    own_head = (row[:, None] // DK == np.arange(P // DK)[None, :]).astype(np.float32)
    own_half = ((np.arange(D)[None, :] // DK) % 2 == row[:, None] // KEYS).astype(np.float32)
    den = np.zeros((P, 2, 2, 2, 8), np.float32)
    for m in range(2):
        for hh in range(2):
            den[hh * KEYS:(hh + 1) * KEYS, m, m, hh, :] = 1.0
    f32 = np.concatenate([ident, own_head, own_half, den.reshape(P, 64)], 1)
    shift = np.zeros((P, pairs, 2, KEYS), np.float32)
    for p in range(pairs):
        for hh in range(2):
            shift[np.arange(KEYS), p, hh, np.arange(KEYS)] = 1.0
            shift[KEYS + 2 * p + hh, p, hh, :] = 1.0
            shift[KEYS + H + 2 * p + hh, p, hh, :] = 1.0
    b16 = np.concatenate([ident, shift.reshape(P, -1), np.ones((P, P), np.float32)], 1)
    return np.ascontiguousarray(f32), np.ascontiguousarray(b16)


def build(nc, x, mask, mask_t, ctx_t, ctx_v, wq_t, bq_col, bq_row, wo_t, bo_row, gates, w_ffn, s_in, s_k, bias_row,
          const_f32, const_b16, out):
    B, S, D = x.shape
    KEYS = mask.shape[2]
    H = 16
    DK = D // H
    TILES = S // P
    HALVES = D // P
    HPH = P // DK
    GROUPS = 4
    SHIFT_ROWS = KEYS + 2 * H
    assert (S, D, KEYS, DK, HALVES) == (512, 256, 64, 16, 2) and B % 2 == 0

    with ExitStack() as ctx:
        def sb(name, shape, dt=F32):
            return ctx.enter_context(nc.sbuf_tensor(name, shape, dt))

        def sem(name):
            return ctx.enter_context(nc.semaphore(name))

        cf = sb("cf", [P, P + HPH + D + 64])
        ident = cf[:, 0:P]
        own_head = cf[:, P:P + HPH]
        own_half = cf[:, P + HPH:P + HPH + D]
        den_w = cf[:, P + HPH + D:P + HPH + D + 64].rearrange("p (m c) -> p m c", m=2)
        cb32 = sb("cb32", [P, P + 8 * P + P])
        cb = sb("cb", [P, P + 8 * P + P], BF16)
        ident_b = cb[:, 0:P]
        shift_w = cb[:, P:9 * P].rearrange("p (g c) -> p g c", g=8)
        ones_b = cb[:, 9 * P:10 * P]
        wq = sb("wq", [P, HALVES, D])
        wq_hi = sb("wq_hi", [P, HALVES, D], F32R)
        wq_lo = sb("wq_lo", [P, HALVES, D], F32R)
        wo = sb("wo", [P, HALVES, D])
        wo_hi = sb("wo_hi", [P, HALVES, D], F32R)
        wo_lo = sb("wo_lo", [P, HALVES, D], F32R)
        bq = sb("bq", [P, HALVES])
        bq_half = sb("bq_half", [P, D])
        bo_tg = sb("bo_tg", [P, D])
        gate = sb("gate", [P, 2])
        tgate = sb("tgate", [P, 2])
        scale_in = sb("scale_in", [P, 2])
        sc = sb("sc", [P, 8])
        wf = sb("wf", [P, HALVES, D], BF16)
        wf_f = sb("wf_f", [P, HALVES, D])
        wf_c = sb("wf_c", [P, HALVES, D])
        wf_8 = sb("wf_8", [P, HALVES, D], FP8)
        wf_8h = sb("wf_8h", [P, HALVES, D], FP8)
        wf_e = sb("wf_e", [P, HALVES, D])
        wf_q = sb("wf_q", [P, HALVES, D], BF16)
        bias_b = sb("bias_b", [P, D], BF16)
        ctxT = sb("ctxT", [P, HALVES, B * KEYS])
        kT = sb("kT", [P, HALVES, B * KEYS])
        kT_hi = sb("kT_hi", [P, HALVES, B * KEYS], F32R)
        kT_lo = sb("kT_lo", [P, HALVES, B * KEYS])
        sc_start = sb("sc_start", [P, 1])
        minus_half = sb("minus_half", [P, TILES])

        x_all = sb("x_all", [P, B, TILES, D])
        mask_i = [sb(f"mask_i{p}", [P, TILES, KEYS], I32) for p in range(2)]
        mask_ti = [sb(f"mask_ti{p}", [KEYS, S], I32) for p in range(2)]
        ctx2 = [sb(f"ctx2{p}", [P, HALVES, P]) for p in range(2)]
        stats = sb("stats", [P, TILES, 6])
        mv = sb("mv", [P, TILES, 2])
        vare = sb("vare", [P, TILES])
        rstd = sb("rstd", [P, TILES])
        z = sb("z", [P, TILES, D])
        z_hi = sb("z_hi", [P, HALVES, S], F32R)
        z_lo = sb("z_lo", [P, HALVES, S], F32R)
        flag = sb("flag", [P, S], BF16)
        qf = sb("qf", [P, HALVES, S])
        q_hi = [sb(f"q_hi{p}", [P, HALVES, S], F32R) for p in range(2)]
        q_lo = [sb(f"q_lo{p}", [P, HALVES, S], F32R) for p in range(2)]
        k_hi = [sb(f"k_hi{p}", [P, HALVES, HPH, KEYS], F32R) for p in range(2)]
        k_lo = [sb(f"k_lo{p}", [P, HALVES, HPH, KEYS], F32R) for p in range(2)]
        v_half = sb("v_half", [P, D])
        v_blk = [sb(f"v_blk{p}", [P, D]) for p in range(2)]
        mbias = sb("mbias", [P, TILES, KEYS], BF16)
        shift = [sb(f"shift{p}", [SHIFT_ROWS, S], BF16) for p in range(2)]
        negmax = sb("negmax", [P, TILES, H])
        negmax_b = sb("negmax_b", [P, TILES, 2, H], BF16)

        probs = sb("probs", [P, 2 * GROUPS, S])
        pv = sb("pv", [P, HALVES, S])
        den = sb("den", [P, S])

        rden = sb("rden", [P, TILES * H])
        rden_x = sb("rden_x", [P, TILES, HALVES, P])
        att = sb("att", [P, HALVES, S])
        att_hi = sb("att_hi", [P, HALVES, S], F32R)
        att_lo = sb("att_lo", [P, HALVES, S], F32R)
        x1 = sb("x1", [P, TILES, D])
        stats2 = sb("stats2", [P, TILES, 6])
        mv2 = sb("mv2", [P, TILES, 2])
        vare2 = sb("vare2", [P, TILES])
        rstd2 = sb("rstd2", [P, TILES])
        u = sb("u", [P, TILES, D], BF16)
        u8 = sb("u8", [P, HALVES, S], FP8)
        y = sb("y", [P, TILES, D], BF16)
        yb = sb("yb", [P, TILES, D], BF16)

        score = [ctx.enter_context(nc.psum_tensor(f"score{s}", [P, 2 * S], F32)) for s in range(2)]
        pv_ps = ctx.enter_context(nc.psum_tensor("pv_ps", [P, S], F32))
        den_ps = ctx.enter_context(nc.psum_tensor("den_ps", [P, S], F32))
        front_ps = ctx.enter_context(nc.psum_tensor("front_ps", [P, S], F32))
        rear_ps = ctx.enter_context(nc.psum_tensor("rear_ps", [P, S], F32))
        front_b = front_ps[:, :].bitcast(BF16)
        rear_b = rear_ps[:, :].bitcast(BF16)

        w_loaded = sem("w_loaded")
        x_loaded = [sem(f"x_loaded{p}") for p in range(2)]
        m_loaded = [sem(f"m_loaded{p}") for p in range(2)]
        w_ready = sem("w_ready")
        wd_step = sem("wd_step")
        wa_ready = sem("wa_ready")
        wp_ready = sem("wp_ready")
        kt_done = sem("kt_done")
        stats_done = sem("stats_done")
        mv_done = sem("mv_done")
        vare_done = sem("vare_done")
        rstd_done = sem("rstd_done")
        z_ready = sem("z_ready")
        zt_done = sem("zt_done")
        zhi_ready = sem("zhi_ready")
        zlo_ready = sem("zlo_ready")
        mb_ready = sem("mb_ready")
        mt_ready = sem("mt_ready")
        masked_counted = sem("masked_counted")
        flag_ready = sem("flag_ready")
        q_done = sem("q_done")
        qf_ready = sem("qf_ready")
        qhi_ready = sem("qhi_ready")
        qlo_ready = sem("qlo_ready")
        khi_ready = sem("khi_ready")
        klo_ready = sem("klo_ready")
        v_done = sem("v_done")
        vhalf_ready = sem("vhalf_ready")
        vblk_ready = sem("vblk_ready")
        a_done = sem("a_done")
        max_done = sem("max_done")
        nmhi_ready = sem("nmhi_ready")
        nm_ready = sem("nm_ready")
        nmt_done = sem("nmt_done")
        shift_ready = sem("shift_ready")
        b_done = sem("b_done")
        exp_done = sem("exp_done")
        pv_done = sem("pv_done")
        pv_copied = sem("pv_copied")
        den_copied = sem("den_copied")
        dent_done = sem("dent_done")
        rden_ready = sem("rden_ready")
        rdenx_ready = sem("rdenx_ready")
        rdent_done = sem("rdent_done")
        att_ready = sem("att_ready")
        atthi_ready = sem("atthi_ready")
        attlo_ready = sem("attlo_ready")
        wo_done = sem("wo_done")
        xres_ready = sem("xres_ready")
        x1_ready = sem("x1_ready")
        stats2_done = sem("stats2_done")
        mv2_done = sem("mv2_done")
        vare2_done = sem("vare2_done")
        rstd2_done = sem("rstd2_done")
        u_ready = sem("u_ready")
        ut_done = sem("ut_done")
        u8_ready = sem("u8_ready")
        y_done = sem("y_done")
        y_ready = sem("y_ready")
        yb_ready = sem("yb_ready")
        out_ready = sem("out_ready")
        stored = sem("stored")

        N_LOADS = 13

        def wait(eng, s, n):
            if not (isinstance(n, int) and n <= 0):
                eng.wait_ge(s, n)

        def wait_all(eng, first, *rest):
            rest = [(s, n) for s, n in rest if not (isinstance(n, int) and n <= 0)]
            for _, n in rest:
                if not isinstance(n, int):
                    eng.compute_val(n)
            eng.wait_ge(*first)
            for s, n in rest:
                eng.wait_ge(s, n)

        def all_iterations(eng, iteration):
            iteration(-1, 1, front=True, current=False, rear=False)
            iteration(0, 0, front=True, current=True, rear=False)
            with eng.Fori(0, (B - 2) // 2) as k:
                for h in range(2):
                    iteration(2 * k + (1 + h), (1 + h) % 2, front=True, current=True, rear=True)
            iteration(B - 1, 1, front=False, current=True, rear=True)
            iteration(B, 0, front=False, current=False, rear=True)

        block = ctx.enter_context(nc.Block())

        @block.sync
        def _(sp):
            sp.dma_start(x_all[:, 0], x[0].rearrange("(t p) d -> p t d", p=P)).then_inc(x_loaded[0], 16)
            sp.dma_start(cf[:], const_f32).then_inc(w_loaded, 16)
            sp.dma_start(ctxT[:], ctx_t.rearrange("(k p) n -> p k n", p=P)).then_inc(w_loaded, 16)
            sp.dma_start(wq[:], wq_t.rearrange("(k p) n -> p k n", p=P)).then_inc(w_loaded, 16)
            sp.dma_start(bq[:], bq_col).then_inc(w_loaded, 16)
            sp.dma_start(bq_half[:], bq_row.broadcast_to((P, D))).then_inc(w_loaded, 16)
            sp.dma_start(gate[:], gates.broadcast_to((P, 2))).then_inc(w_loaded, 16)
            sp.dma_start(cb32[:], const_b16).then_inc(w_loaded, 16)

            def batch_loads(b, p):
                sp.dma_start(mask_i[p][:], mask[b].rearrange("a (t p) j -> p (a t) j", p=P)).then_inc(m_loaded[p], 16)
                sp.dma_start(mask_ti[p][:], mask_t[b].rearrange("a j s -> j (a s)")).then_inc(m_loaded[p], 16)
                sp.dma_start(ctx2[p][:], ctx_v[b].rearrange("a (k p) n -> p (a k) n", p=P)).then_inc(m_loaded[p], 16)

            def x_load(b, p):
                sp.dma_start(x_all[:, b], x[b].rearrange("a (t p) d -> p a t d", p=P)).then_inc(x_loaded[p], 16)

            batch_loads(bass.ds(0, 1), 0)
            sp.dma_start(bo_tg[:], bo_row.broadcast_to((P, D))).then_inc(w_loaded, 16)
            sp.dma_start(wo[:], wo_t.rearrange("(k p) n -> p k n", p=P)).then_inc(w_loaded, 16)
            sp.dma_start(wf[:], w_ffn.rearrange("(k p) n -> p k n", p=P)).then_inc(w_loaded, 16)
            sp.dma_start(scale_in[:, 0:1], s_in.broadcast_to((P, 1))).then_inc(w_loaded, 16)
            sp.dma_start(scale_in[:, 1:2], s_k.broadcast_to((P, 1))).then_inc(w_loaded, 16)
            sp.dma_start(bias_b[:], bias_row.broadcast_to((P, D))).then_inc(w_loaded, 16)
            x_load(bass.ds(1, 1), 1)
            batch_loads(bass.ds(1, 1), 1)
            assert N_LOADS == 7 + 6

            def next_loads(b, k, p):
                wait_all(sp, (w_loaded, 16 * N_LOADS), (x_loaded[p], 16 * k), (m_loaded[p], 48 * k))
                x_load(bass.ds(b, 1), p)
                wait_all(sp, (w_loaded, 16 * N_LOADS), (mb_ready, b - 1), (mt_ready, b - 1), (v_done, b - 1))
                batch_loads(bass.ds(b, 1), p)

            def store(b):
                sp.wait_ge(out_ready, 2 * b + 2)
                sp.dma_start(out[bass.ds(b, 1)].rearrange("a (t p) d -> p a t d", p=P),
                             x_all[:, bass.ds(b, 1)]).then_inc(stored, 16)

            next_loads(2, 1, 0)
            with sp.Fori(0, (B - 4) // 2) as k:
                for h in range(2):
                    next_loads(2 * k + 3 + h, k + 1 + h, (1 + h) % 2)
                    store(2 * k + h)
            next_loads(B - 1, B // 2 - 1, 1)
            for b in range(B - 4, B):
                store(b)
            sp.wait_ge(stored, 16 * B)

        @block.gpsimd
        def _(pool):
            pool.memset(minus_half[:], -0.5).then_inc(wp_ready, 1)
            pool.wait_ge(w_loaded, 16 * N_LOADS)
            pool.tensor_tensor(bq_half[:], bq_half[:], own_half, ALU.mult).then_inc(wp_ready, 1)
            pool.wait_ge(wa_ready, 1)
            pool.tensor_scalar(bo_tg[:], bo_tg[:], tgate[:, 0:1], None, ALU.mult).then_inc(wp_ready, 1)
            pool.wait_ge(wp_ready, 3)

            def iteration(i, pc, front, current, rear):
                f, r = i + 1, i - 1
                pf = 1 - pc
                if front:
                    wait_all(pool, (wp_ready, 3),
                             (m_loaded[pf], 48 * ((f - pf) // 2 + 1) if isinstance(f, int) else 24 * (f - pf) + 48),
                             (a_done, 4 * f))
                    pool.tensor_scalar(mbias[:], mask_i[pf][:], 0.0, MASKED, ALU.is_equal, ALU.mult).then_inc(mb_ready, 1)
                    wait_all(pool, (wp_ready, 3),
                             (b_done, 4 * f - 4))
                    pool.tensor_scalar(shift[pf][0:KEYS, :], mask_ti[pf][:], 0.0, MASKED, ALU.is_equal,
                                       ALU.mult).then_inc(mt_ready, 1)
                    wait_all(pool, (wp_ready, 3),
                             (mv_done, f + 1),
                             (z_ready, f))
                    pool.tensor_scalar(vare[:], mv[:, :, 1], EPS, None, ALU.add).then_inc(vare_done, 1)
                    wait(pool, vare_done, f + 1)
                    pool.tensor_tensor(rstd[:], vare[:], minus_half[:], ALU.pow).then_inc(rstd_done, 1)
                    if isinstance(f, int) and f == 0:
                        wait(pool, w_ready, 8)
                    for m in range(HALVES):
                        kin = kT[:, m, bass.ds(f * KEYS, KEYS)].unsqueeze(1).broadcast_to((P, HPH, KEYS))
                        ins = pool.tensor_tensor(k_hi[pf][:, m], kin, own_head.unsqueeze(2).broadcast_to((P, HPH, KEYS)),
                                                 ALU.mult)
                    ins.then_inc(khi_ready, 1)
                if rear:
                    for m in range(HALVES):
                        wait(pool, atthi_ready, 2 * r + m + 1)
                        pool.tensor_tensor(att_lo[:, m], att[:, m], att_hi[:, m].bitcast(F32),
                                           ALU.subtract).then_inc(attlo_ready, 1)
                if front:
                    for m in range(HALVES):
                        kin = kT_lo[:, m, bass.ds(f * KEYS, KEYS)].unsqueeze(1).broadcast_to((P, HPH, KEYS))
                        ins = pool.tensor_tensor(k_lo[pf][:, m], kin, own_head.unsqueeze(2).broadcast_to((P, HPH, KEYS)),
                                                 ALU.mult)
                    ins.then_inc(klo_ready, 1)
                    wait(pool, z_ready, f + 1)
                    xb = x_all[:, bass.ds(f, 1)].rearrange("p a t d -> p (a t) d")
                    pool.tensor_tensor(xb, xb, bo_tg[:].unsqueeze(1).broadcast_to((P, TILES, D)),
                                       ALU.add).then_inc(xres_ready, 1)
                    for m in range(HALVES):
                        wait(pool, qhi_ready, 2 * f + m + 1)
                        pool.tensor_tensor(q_lo[pf][:, m], qf[:, m], q_hi[pf][:, m].bitcast(F32),
                                           ALU.subtract).then_inc(qlo_ready, 1)
                        if m == 0 and rear:
                            wait_all(pool, (wp_ready, 3),
                                     (mv2_done, r + 1))
                            pool.tensor_scalar(vare2[:], mv2[:, :, 1], EPS, None, ALU.add).then_inc(vare2_done, 1)
                            wait(pool, vare2_done, r + 1)
                            pool.tensor_tensor(rstd2[:], vare2[:], minus_half[:], ALU.pow).then_inc(rstd2_done, 1)
                    wait(pool, vhalf_ready, f + 1)
                    wait(pool, pv_done, 4 * f - 4)
                    pool.tensor_tensor(v_blk[pf][:], v_half[:], bq_half[:], ALU.add).then_inc(vblk_ready, 1)
                elif rear:
                    wait_all(pool, (wp_ready, 3),
                             (mv2_done, r + 1))
                    pool.tensor_scalar(vare2[:], mv2[:, :, 1], EPS, None, ALU.add).then_inc(vare2_done, 1)
                    wait(pool, vare2_done, r + 1)
                    pool.tensor_tensor(rstd2[:], vare2[:], minus_half[:], ALU.pow).then_inc(rstd2_done, 1)
                if rear:
                    for h in range(2):
                        wait(pool, y_ready, 2 * r + h + 2)
                        pool.tensor_tensor(yb[:, 2 * h:2 * h + 2], y[:, 2 * h:2 * h + 2],
                                           bias_b[:].unsqueeze(1).broadcast_to((P, 2, D)),
                                           ALU.add).then_inc(yb_ready, 1)

            all_iterations(pool, iteration)

        @block.scalar
        def _(act):
            act.wait_ge(w_loaded, 16 * N_LOADS)
            nc.scalar.activation(tgate[:], gate[:], ACT.Tanh).then_inc(wa_ready, 1)
            nc.scalar.activation(wq_hi[:], wq[:], ACT.Copy).then_inc(wa_ready, 1)
            nc.scalar.activation(cb[:], cb32[:], ACT.Copy).then_inc(wa_ready, 1)
            nc.scalar.activation(wo_hi[:], wo[:], ACT.Copy).then_inc(wa_ready, 1)
            act.wait_ge(w_ready, 6)
            nc.scalar.activation(kT_hi[:], kT[:], ACT.Copy).then_inc(wa_ready, 1)
            act.wait_ge(wa_ready, 5)
            nc.scalar.activation(sc_start[:], kT[:, 0, 0:1], ACT.Copy).then_inc(y_ready, 1)
            act.wait_ge(w_ready, 9)

            def z_high(f, m):
                wait(act, zt_done, 2 * f + m + 1)
                wait(act, q_done, 2 * f)
                nc.scalar.activation(z_hi[:, m], front_ps[:, :], ACT.Copy).then_inc(zhi_ready, 1)

            def q_high(f, p, m):
                wait(act, qf_ready, 2 * f + m + 1)
                wait(act, b_done, 4 * f - 4)
                nc.scalar.activation(q_hi[p][:, m], qf[:, m], ACT.Copy).then_inc(qhi_ready, 1)

            def exp(c, g):
                wait(act, b_done, 4 * c + g + 1)
                wait(act, pv_done, 4 * c + g - 3)
                nc.scalar.activation(probs[:, 2 * g:2 * g + 2], score[g % 2][:, :].rearrange("p (a s) -> p a s", a=2),
                                     ACT.Exp, scale=float(DK) ** -0.5).then_inc(exp_done, 1)

            def pv_copy(c, m):
                wait(act, pv_done, 4 * c + 2 * m + 2)
                wait(act, att_ready, 2 * c)
                nc.scalar.activation(pv[:, m], pv_ps[:, :], ACT.Copy).then_inc(pv_copied, 1)

            def att_high(r, m):
                wait(act, att_ready, 2 * r + m + 1)
                nc.scalar.activation(att_hi[:, m], att[:, m], ACT.Copy).then_inc(atthi_ready, 1)

            def y_scale(r, h):
                wait(act, y_done, 2 * r + h + 1)
                nc.scalar.activation(y[:, 2 * h:2 * h + 2], rear_ps[:, :].rearrange("p (a d) -> p a d", a=2), ACT.Copy,
                                     scale=sc[:, 4:5]).then_inc(y_ready, 1)

            def iteration(i, pc, front, current, rear):
                c, f, r = i, i + 1, i - 1
                pf = 1 - pc
                if current:
                    exp(c, 0)
                if rear:
                    wait(act, rden_ready, r + 1)
                    nc.scalar.activation(rden_x[:].rearrange("p t m (h e) -> p (t m h) e", e=DK),
                                         rden[:].unsqueeze(2).broadcast_to((P, TILES * H, DK)),
                                         ACT.Copy).then_inc(rdenx_ready, 1)
                if current:
                    exp(c, 1)
                if rear:
                    att_high(r, 0)
                if front:
                    z_high(f, 0)
                if rear:
                    att_high(r, 1)
                if current:
                    exp(c, 2)
                    pv_copy(c, 0)
                if front:
                    z_high(f, 1)
                if current:
                    exp(c, 3)
                if front:
                    q_high(f, pf, 0)
                if current:
                    pv_copy(c, 1)
                    wait(act, pv_done, 4 * c + 4)
                    wait(act, dent_done, c)
                    nc.scalar.activation(den[:], den_ps[:, :], ACT.Copy).then_inc(den_copied, 1)
                if front:
                    q_high(f, pf, 1)
                if rear:
                    wait_all(act, (w_ready, 9),
                             (ut_done, r + 1))
                    nc.scalar.activation(u8[:], rear_b.rearrange("p (m s) -> p m s", m=HALVES), ACT.Copy,
                                         scale=sc[:, 3:4], saturate=False).then_inc(u8_ready, 1)
                    y_scale(r, 0)
                if front:
                    wait(act, nmt_done, f + 1)
                    wait(act, b_done, 4 * f - 4)
                    nc.scalar.activation(shift[pf][KEYS:SHIFT_ROWS, :], front_b[KEYS:SHIFT_ROWS, 0:S],
                                         ACT.Copy).then_inc(shift_ready, 1)
                if rear:
                    y_scale(r, 1)

            all_iterations(act, iteration)

        @block.vector
        def _(dve):
            dve.wait_ge(wa_ready, 2)
            nc.vector.tensor_tensor(wq_lo[:], wq[:], wq_hi[:].bitcast(F32), ALU.subtract).then_inc(w_ready, 1)
            dve.wait_ge(wa_ready, 4)
            nc.vector.tensor_tensor(wo_lo[:], wo[:], wo_hi[:].bitcast(F32), ALU.subtract).then_inc(w_ready, 1)
            nc.vector.reciprocal(sc[:, 0:2], scale_in[:]).then_inc(w_ready, 1)
            dve.wait_ge(w_ready, 3)
            nc.vector.tensor_scalar(sc[:, 5:6], sc[:, 0:1], sc[:, 0:1], None, ALU.mult).then_inc(w_ready, 1)
            for m in range(HALVES):
                dve.wait_ge(kt_done, m + 1)
                nc.vector.tensor_scalar(kT[:, m], score[0][:, m * S:(m + 1) * S], bq[:, m:m + 1], None,
                                        ALU.add).then_inc(w_ready, 1)
            dve.wait_ge(w_ready, 6)
            nc.vector.tensor_scalar(sc[:, 2:3], sc[:, 5:6], FP8_MAX ** 2 / D, None, ALU.is_gt).then_inc(w_ready, 1)
            dve.wait_ge(wa_ready, 5)
            nc.vector.tensor_tensor(kT_lo[:], kT[:], kT_hi[:].bitcast(F32), ALU.subtract).then_inc(w_ready, 1)
            dve.wait_ge(w_ready, 8)
            nc.vector.tensor_scalar(sc[:, 6:7], sc[:, 2:3], -0.5, 1.0, ALU.mult, ALU.add)
            nc.vector.tensor_scalar(sc[:, 7:8], sc[:, 2:3], 1.0, None, ALU.add)
            nc.vector.tensor_scalar(sc[:, 5:6], scale_in[:, 0:1], scale_in[:, 1:2], None, ALU.mult).then_inc(wd_step, 1)
            dve.wait_ge(wd_step, 1)
            nc.vector.tensor_scalar(sc[:, 3:4], sc[:, 0:1], sc[:, 6:7], None, ALU.mult)
            nc.vector.tensor_scalar(sc[:, 4:5], sc[:, 5:6], sc[:, 7:8], None, ALU.mult).then_inc(w_ready, 1)
            nc.vector.tensor_scalar(wf_f[:], wf[:], sc[:, 1:2], None, ALU.mult).then_inc(wd_step, 1)
            dve.wait_ge(wd_step, 2)
            nc.vector.tensor_scalar(wf_c[:], wf_f[:], FP8_MAX, -FP8_MAX, ALU.min, ALU.max).then_inc(wd_step, 1)
            dve.wait_ge(wd_step, 3)
            nc.vector.tensor_copy(wf_8[:], wf_c[:], saturate=False)
            nc.vector.tensor_scalar(wf_8h[:], wf_f[:], 0.5, None, ALU.mult, saturate=False).then_inc(wd_step, 1)
            dve.wait_ge(wd_step, 4)
            nc.vector.tensor_scalar(wf_f[:], wf_8h[:], 2.0, None, ALU.mult)
            nc.vector.tensor_scalar(wf_c[:], wf_8h[:], FP8_MAX / 2, -FP8_MAX / 2, ALU.min, ALU.max).then_inc(wd_step, 1)
            dve.wait_ge(wd_step, 5)
            nc.vector.scalar_tensor_tensor(wf_e[:].rearrange("p a b -> p (a b)"), wf_c[:].rearrange("p a b -> p (a b)"),
                                           -2.0, wf_f[:].rearrange("p a b -> p (a b)"), ALU.mult,
                                           ALU.add).then_inc(wd_step, 1)
            dve.wait_ge(wd_step, 6)
            nc.vector.tensor_tensor(wf_q[:], wf_8[:], wf_e[:], ALU.add).then_inc(w_ready, 1)

            def layer_norm_stats(src, st, agg, n, first_done, second_done):
                for t in range(TILES):
                    ins = nc.vector.bn_stats(st[:, t], src[:, t])
                ins.then_inc(first_done, 1)
                wait_all(dve, (w_ready, 10),
                         (first_done, n + 1))
                for t in range(TILES):
                    ins = nc.vector.bn_aggr(agg[:, t], st[:, t])
                ins.then_inc(second_done, 1)

            def z_low(f, m):
                wait(dve, zhi_ready, 2 * f + m + 1)
                wait(dve, q_done, 2 * f)
                nc.vector.tensor_tensor(z_lo[:, m], front_ps[:, :], z_hi[:, m].bitcast(F32),
                                        ALU.subtract).then_inc(zlo_ready, 1)

            def q_float(f, m):
                wait(dve, q_done, 2 * f + m + 1)
                wait(dve, flag_ready, f + 1)
                wait(dve, qlo_ready, 2 * f)
                nc.vector.scalar_tensor_tensor(qf[:, m], front_ps[:, :], bq[:, m:m + 1], flag[:], ALU.add,
                                               ALU.mult).then_inc(qf_ready, 1)

            def attend(r, m):
                wait(dve, rdent_done, 2 * r + m + 1)
                nc.vector.tensor_tensor(att[:, m], rear_ps[:, :], pv[:, m], ALU.mult).then_inc(att_ready, 1)

            def residual(r, h):
                wait(dve, wo_done, 2 * r + h + 1)
                wait(dve, xres_ready, r + 1)
                xb = x_all[:, bass.ds(r, 1), 2 * h:2 * h + 2].rearrange("p a t d -> p (a t d)")
                nc.vector.scalar_tensor_tensor(x1[:, 2 * h:2 * h + 2].rearrange("p t d -> p (t d)"), rear_ps[:, :],
                                               tgate[:, 0:1], xb, ALU.mult, ALU.add).then_inc(x1_ready, 1)

            def row_max(f, t):
                wait(dve, a_done, 4 * f + t + 1)
                nc.vector.tensor_reduce(negmax[:, t], score[t % 2][:, :].rearrange("p (h j) -> p h j", h=H), AX_X,
                                        ALU.max, negate=True).then_inc(max_done, 1)

            def iteration(i, pc, front, current, rear):
                c, f, r = i, i + 1, i - 1
                pf = 1 - pc
                if front:
                    n = 16 * ((f - pf) // 2 + 1) if isinstance(f, int) else 8 * (f - pf) + 16
                    wait(dve, x_loaded[pf], n)
                    xb = x_all[:, bass.ds(f, 1)].rearrange("p a t d -> p (a t) d")
                    layer_norm_stats(xb, stats, mv, f, stats_done, mv_done)
                if rear:
                    wait(dve, dent_done, r + 1)
                    src = rear_ps[:, :].rearrange("p (t a b m h e) -> p t a b m h e", t=TILES, a=2, b=2, m=2, h=2)
                    dst = rden[:].rearrange("p (t m a b h) -> p t m a b h", t=TILES, m=2, a=2, b=2)
                    for a in range(2):
                        for m in range(HALVES):
                            ins = nc.vector.reciprocal(dst[:, :, m, a], src[:, :, 1 - a, :, m, :, 0])
                    ins.then_inc(rden_ready, 1)
                if front:
                    wait(dve, masked_counted, f + 1)
                    nc.vector.tensor_scalar(flag[:], front_ps[:, :], KEYS * MASKED, None,
                                            ALU.not_equal).then_inc(flag_ready, 1)
                    wait(dve, rstd_done, f + 1)
                    wait(dve, zt_done, 2 * f)
                    for t in range(TILES):
                        ins = nc.vector.tensor_scalar(z[:, t], xb[:, t], mv[:, t, 0:1], rstd[:, t:t + 1], ALU.subtract,
                                                      ALU.mult)
                    ins.then_inc(z_ready, 1)
                if rear:
                    attend(r, 0)
                if front:
                    z_low(f, 0)
                if rear:
                    attend(r, 1)
                if front:
                    z_low(f, 1)
                if rear:
                    residual(r, 0)
                if front:
                    q_float(f, 0)
                if rear:
                    residual(r, 1)
                if front:
                    q_float(f, 1)
                if rear:
                    wait(dve, x1_ready, 2 * r + 2)
                    layer_norm_stats(x1, stats2, mv2, r, stats2_done, mv2_done)
                if front:
                    wait(dve, v_done, f + 1)
                    wait(dve, vblk_ready, f)
                    nc.vector.tensor_tensor(v_half[:], front_ps[:, 0:D], own_half, ALU.mult).then_inc(vhalf_ready, 1)
                    row_max(f, 0)
                    row_max(f, 1)
                if rear:
                    wait(dve, rstd2_done, r + 1)
                    for t in range(TILES):
                        ins = nc.vector.tensor_scalar(u[:, t], x1[:, t], mv2[:, t, 0:1], rstd2[:, t:t + 1],
                                                      ALU.subtract, ALU.mult)
                    ins.then_inc(u_ready, 1)
                if front:
                    row_max(f, 2)
                    row_max(f, 3)
                    wait(dve, max_done, 4 * f + 4)
                    wait(dve, nmt_done, f)
                    nc.vector.tensor_copy(negmax_b[:, :, 0], negmax[:]).then_inc(nmhi_ready, 1)
                    wait(dve, nmhi_ready, f + 1)
                    nc.vector.tensor_tensor(negmax_b[:, :, 1], negmax[:], negmax_b[:, :, 0],
                                            ALU.subtract).then_inc(nm_ready, 1)
                if rear:
                    for h in range(2):
                        wait(dve, yb_ready, 2 * r + h + 1)
                        sl = slice(2 * h, 2 * h + 2)
                        nc.vector.scalar_tensor_tensor(
                            x_all[:, bass.ds(r, 1), sl].rearrange("p a t d -> p (a t d)"), yb[:, sl].rearrange("p t d -> p (t d)"),
                            tgate[:, 1:2], x1[:, sl].rearrange("p t d -> p (t d)"), ALU.mult,
                            ALU.add).then_inc(out_ready, 1)

            all_iterations(dve, iteration)

        @block.tensor
        def _(pe):
            mm = nc.tensor.matmul

            pe.wait_ge(w_loaded, 16 * N_LOADS)
            for m in range(HALVES):
                for k in range(HALVES):
                    ins = mm(score[0][:, m * S:(m + 1) * S], wq[:, k, m * P:(m + 1) * P], ctxT[:, k], start=(k == 0),
                             stop=(k == HALVES - 1))
                ins.then_inc(kt_done, 1)
            pe.wait_ge(w_ready, 6)
            pe.wait_ge(wa_ready, 4)

            def count_masked(f, p):
                wait(pe, mt_ready, f + 1)
                wait(pe, shift_ready, f)
                mm(front_ps[:, :], ones_b[0:KEYS], shift[p][0:KEYS], start=True, stop=True).then_inc(masked_counted, 1)

            def z_transpose(f, m):
                wait(pe, z_ready, f + 1)
                if m == 0:
                    wait(pe, flag_ready, f + 1)
                else:
                    wait(pe, zlo_ready, 2 * f + 1)
                for t in range(TILES):
                    ins = nc.tensor.transpose(front_ps[:, t * P:(t + 1) * P], z[:, t, m * P:(m + 1) * P], ident)
                ins.then_inc(zt_done, 1)

            def q_project(f, m):
                wait(pe, zlo_ready, 2 * f + 2)
                if m == 1:
                    wait(pe, qf_ready, 2 * f + 1)
                steps = [(a, b, k) for k in range(HALVES) for a, b in ((wq_hi, z_hi), (wq_lo, z_hi), (wq_hi, z_lo))]
                for n, (a, b, k) in enumerate(steps):
                    ins = mm(front_ps[:, :], a[:, k, m * P:(m + 1) * P], b[:, k], start=(n == 0),
                             stop=(n == len(steps) - 1))
                ins.then_inc(q_done, 1)

            def v_project(f, p):
                wait(pe, qf_ready, 2 * f + 2)
                wait(pe, m_loaded[p], 48 * ((f - p) // 2 + 1) if isinstance(f, int) else 24 * (f - p) + 48)
                for k in range(HALVES):
                    ins = mm(front_ps[:, 0:D], ctx2[p][:, k], wq[:, k], start=(k == 0), stop=(k == HALVES - 1))
                ins.then_inc(v_done, 1)

            def scores_by_query(f, p, t):
                wait(pe, qhi_ready, 2 * f + 2)
                wait(pe, khi_ready, f + 1)
                wait(pe, mb_ready, f + 1)
                if t < 2:
                    wait(pe, exp_done, 4 * f - 1 + t)
                    if isinstance(f, int) and f == 0 and t == 0:
                        wait(pe, w_ready, 6)
                else:
                    wait(pe, max_done, 4 * f + t - 1)
                for m in range(HALVES):
                    dst = score[t % 2][:, m * S:(m + 1) * S]
                    mm(dst, q_hi[p][:, m, t * P:(t + 1) * P], k_hi[p][:, m].rearrange("p h j -> p (h j)"), start=True,
                       stop=False)
                    ins = mm(dst, ident_b, mbias[:, t].unsqueeze(1).broadcast_to((P, HPH, KEYS)), start=False, stop=True)
                ins.then_inc(a_done, 1)

            def negmax_transpose(f):
                wait(pe, nm_ready, f + 1)
                wait(pe, vhalf_ready, f + 1)
                for t in range(TILES):
                    ins = nc.tensor.transpose(front_b[KEYS:SHIFT_ROWS, t * P:(t + 1) * P],
                                              negmax_b[:, t].rearrange("p a h -> p (a h)"), ident_b)
                ins.then_inc(nmt_done, 1)

            def scores_by_key(c, p, g):
                wait(pe, qlo_ready, 2 * c + 2)
                wait(pe, klo_ready, c + 1)
                wait(pe, shift_ready, c + 1)
                if g < 2:
                    wait(pe, max_done, 4 * c + g + 3)
                else:
                    wait(pe, exp_done, 4 * c + g - 1)
                for n in range(2):
                    pair = 2 * g + n
                    m, j = divmod(pair, 4)
                    dst = score[g % 2][:, n * S:(n + 1) * S]
                    for a, (kk, q) in enumerate(((k_hi, q_hi), (k_lo, q_hi), (k_hi, q_lo))):
                        mm(dst, kk[p][:, m, 2 * j:2 * j + 2].rearrange("p h j -> p (h j)"), q[p][:, m], start=(a == 0),
                           stop=False)
                    ins = mm(dst, shift_w[0:SHIFT_ROWS, pair], shift[p][:], start=False, stop=True)
                ins.then_inc(b_done, 1)

            def weigh_values(c, p, g):
                wait(pe, exp_done, 4 * c + g + 1)
                wait(pe, vblk_ready, c + 1)
                if g == 0:
                    wait(pe, den_copied, c)
                if g % 2 == 0:
                    wait(pe, pv_copied, 2 * c + g // 2)
                for n in range(2):
                    pair = 2 * g + n
                    m, j = divmod(pair, 4)
                    mm(pv_ps[32 * j:32 * j + 32, :], v_blk[p][:, 32 * pair:32 * pair + 32], probs[:, pair], start=True,
                       stop=True)
                for n in range(2):
                    pair = 2 * g + n
                    m, j = divmod(pair, 4)
                    jd = (j + 2) % 4
                    ins = mm(den_ps[32 * jd:32 * jd + 32, :], den_w[:, m], probs[:, pair], start=(m == 0), stop=(m == 1))
                ins.then_inc(pv_done, 1)

            def den_transpose(r):
                wait(pe, den_copied, r + 1)
                wait(pe, y_ready, 2 * r + 1)
                for t in range(TILES):
                    ins = nc.tensor.transpose(rear_ps[:, t * P:(t + 1) * P], den[:, t * P:(t + 1) * P], ident)
                ins.then_inc(dent_done, 1)

            def rden_transpose(r, m):
                wait(pe, rdenx_ready, r + 1)
                if m == 1:
                    wait(pe, att_ready, 2 * r + 1)
                for t in range(TILES):
                    ins = nc.tensor.transpose(rear_ps[:, t * P:(t + 1) * P], rden_x[:, t, m], ident)
                ins.then_inc(rdent_done, 1)

            def out_project(r, h):
                wait(pe, attlo_ready, 2 * r + 2)
                if h == 1:
                    wait(pe, x1_ready, 2 * r + 1)
                for t in (2 * h, 2 * h + 1):
                    dst = rear_ps[:, (t % 2) * D:(t % 2 + 1) * D]
                    steps = [(a, w, m) for m in range(HALVES)
                             for a, w in ((att_hi, wo_hi), (att_lo, wo_hi), (att_hi, wo_lo))]
                    for n, (a, w, m) in enumerate(steps):
                        ins = mm(dst, a[:, m, t * P:(t + 1) * P], w[:, m], start=(n == 0), stop=(n == len(steps) - 1))
                ins.then_inc(wo_done, 1)

            def u_transpose(r):
                wait(pe, u_ready, r + 1)
                wait(pe, x1_ready, 2 * r + 2)
                for m in range(HALVES):
                    for t in range(TILES):
                        ins = nc.tensor.transpose(rear_b[:, m * S + t * P:m * S + (t + 1) * P],
                                                  u[:, t, m * P:(m + 1) * P], ident_b)
                ins.then_inc(ut_done, 1)

            def ffn(r, h):
                if h == 0:
                    wait_all(pe, (w_ready, 10), (u8_ready, r + 1))
                else:
                    wait_all(pe, (w_ready, 10), (y_ready, 2 * r + 2))
                for t in (2 * h, 2 * h + 1):
                    for m in range(HALVES):
                        ins = mm(rear_ps[:, (t % 2) * D:(t % 2 + 1) * D], u8[:, m, t * P:(t + 1) * P], wf_q[:, m],
                                 start=(m == 0), stop=(m == HALVES - 1))
                ins.then_inc(y_done, 1)

            def iteration(i, pc, front, current, rear):
                c, f, r = i, i + 1, i - 1
                pf = 1 - pc
                if rear:
                    den_transpose(r)
                if current:
                    scores_by_key(c, pc, 0)
                if front:
                    count_masked(f, pf)
                if current:
                    scores_by_key(c, pc, 1)
                if rear:
                    rden_transpose(r, 0)
                if current:
                    weigh_values(c, pc, 0)
                if front:
                    z_transpose(f, 0)
                if rear:
                    rden_transpose(r, 1)
                if current:
                    scores_by_key(c, pc, 2)
                    weigh_values(c, pc, 1)
                if front:
                    z_transpose(f, 1)
                if rear:
                    out_project(r, 0)
                if current:
                    scores_by_key(c, pc, 3)
                    weigh_values(c, pc, 2)
                if front:
                    q_project(f, 0)
                if rear:
                    out_project(r, 1)
                if current:
                    weigh_values(c, pc, 3)
                if front:
                    q_project(f, 1)
                    v_project(f, pf)
                    for t in range(TILES):
                        scores_by_query(f, pf, t)
                if rear:
                    u_transpose(r)
                    ffn(r, 0)
                if front:
                    negmax_transpose(f)
                if rear:
                    ffn(r, 1)

            all_iterations(pe, iteration)


_INS = ["x", "mask", "mask_t", "ctx_t", "ctx_v", "wq_t", "bq_col", "bq_row", "wo_t", "bo_row", "gates", "w_ffn", "s_in",
        "s_k", "bias_row", "const_f32", "const_b16"]


def kernel(**inputs):
    import numpy as _np
    import concourse.bacc as _bacc
    from concourse import mybir as _mybir
    from concourse.bass_utils import run_bass_kernel_spmd as _run

    given = {k: _np.asarray(v) for k, v in inputs.items()}
    x, keys = given["x"], given["ctx_1024"]
    batch, seq, dim = x.shape
    n_keys = keys.shape[1]
    mask = given["mask_Bx1xSxS2_if1"].reshape(batch, seq, n_keys)
    f32, b16 = constants(dim, 16, n_keys)
    keys_t = keys.transpose(0, 2, 1)
    laid = {
        "x": x,
        "mask": mask,
        "mask_t": mask.transpose(0, 2, 1),
        "ctx_t": keys_t.transpose(1, 0, 2).reshape(dim, batch * n_keys),
        "ctx_v": _np.concatenate([keys_t, keys_t], 2),
        "wq_t": given["L0_xattn_Wq"].T,
        "bq_col": given["L0_xattn_bq"].reshape(dim // 128, 128).T,
        "bq_row": given["L0_xattn_bq"].reshape(1, dim),
        "wo_t": given["L0_xattn_Wo"].T,
        "bo_row": given["L0_xattn_bo"].reshape(1, dim),
        "gates": _np.concatenate([given["g_xattn"], given["g_ffn"]]).reshape(1, 2),
        "w_ffn": given["L0_ffn_kernel"],
        "s_in": given["L0_ffn_input_scale"].reshape(1, 1),
        "s_k": given["L0_ffn_kernel_scale"].reshape(1, 1),
        "bias_row": given["L0_ffn_bias"].reshape(1, dim),
        "const_f32": f32,
        "const_b16": b16,
    }
    nc = _bacc.Bacc("TRN2", target_bir_lowering=False, num_devices=1)
    arrays, args = {}, []
    for name in _INS:
        a = _np.ascontiguousarray(laid[name])
        arrays[f"in_{name}_dram"] = a
        args.append(nc.dram_tensor(f"in_{name}_dram", a.shape, _mybir.dt.from_np(a.dtype), kind="ExternalInput").ap())
    args.append(nc.dram_tensor("out_0_dram", x.shape, _mybir.dt.from_np(x.dtype), kind="ExternalOutput").ap())
    build(nc, *args)
    return _run(nc, [arrays], core_ids=[0]).results[0]["out_0_dram"]
```

```python
from contextlib import ExitStack

import numpy as np

import concourse.bass as bass
from concourse import mybir

ALU = mybir.AluOpType
ACT = mybir.ActivationFunctionType
AX_X = mybir.AxisListType.X
F32 = mybir.dt.float32
F32R = mybir.dt.float32r
BF16 = mybir.dt.bfloat16
FP8 = mybir.dt.float8e4
I32 = mybir.dt.int32

P = 128
MASKED = -(2.0 ** 100)
EPS = 1e-5
FP8_MAX = 240.0


def constants(D, H, KEYS):
    DK = D // H
    row = np.arange(P)
    pairs = H // 2
    ident = np.eye(P, dtype=np.float32)
    own_head = (row[:, None] // DK == np.arange(P // DK)[None, :]).astype(np.float32)
    own_half = ((np.arange(D)[None, :] // DK) % 2 == row[:, None] // KEYS).astype(np.float32)
    den = np.zeros((P, 2, 2, 2, 8), np.float32)
    for m in range(2):
        for hh in range(2):
            den[hh * KEYS:(hh + 1) * KEYS, m, m, hh, :] = 1.0
    own_in_pair = ((row[:, None] // DK) % 2 == np.arange(2)[None, :]).astype(np.float32)
    f32 = np.concatenate([ident, own_head, own_half, den.reshape(P, 64), own_in_pair], 1)
    shift = np.zeros((P, pairs, 2, KEYS), np.float32)
    for p in range(pairs):
        for hh in range(2):
            shift[np.arange(KEYS), p, hh, np.arange(KEYS)] = 1.0
            shift[KEYS + 2 * p + hh, p, hh, :] = 1.0
            shift[KEYS + H + 2 * p + hh, p, hh, :] = 1.0
    b16 = np.concatenate([ident, shift.reshape(P, -1), np.ones((P, P), np.float32)], 1)
    return np.ascontiguousarray(f32), np.ascontiguousarray(b16)


def build(nc, x, mask, mask_t, ctx_t, wq_t, bq_col, wo_t, bo_row, gates, w_ffn, s_in, s_k, bias_row,
          const_f32, const_b16, out):
    B, S, D = x.shape
    KEYS = mask.shape[2]
    H = 16
    DK = D // H
    TILES = S // P
    HALVES = D // P
    HPH = P // DK
    GROUPS = 4
    SHIFT_ROWS = KEYS + 2 * H
    PAIR = 2 * DK
    STACK = 3 * PAIR
    PAIRS_PER_HALF = P // PAIR
    BO_ROWS = 96
    STAGED = 16 * 3 * PAIRS_PER_HALF
    assert (S, D, KEYS, DK, HALVES) == (512, 256, 64, 16, 2) and B % 2 == 0

    with ExitStack() as ctx:
        def sb(name, shape, dt=F32):
            return ctx.enter_context(nc.sbuf_tensor(name, shape, dt))

        def sem(name):
            return ctx.enter_context(nc.semaphore(name))

        cf = sb("cf", [P, P + HPH + D + 64 + 2])
        ident = cf[:, 0:P]
        own_head = cf[:, P:P + HPH]
        own_half = cf[:, P + HPH:P + HPH + D]
        den_w = cf[:, P + HPH + D:P + HPH + D + 64].rearrange("p (m c) -> p m c", m=2)
        own_in_pair = cf[0:3 * 2 * DK, P + HPH + D + 64:P + HPH + D + 66]
        cb = sb("cb", [P, P + 8 * P + P], BF16)
        ident_b = cb[:, 0:P]
        shift_w = cb[:, P:9 * P].rearrange("p (g c) -> p g c", g=8)
        ones_b = cb[:, 9 * P:10 * P]
        wq = sb("wq", [P, HALVES, D])
        wq_hi = sb("wq_hi", [P, HALVES, D], F32R)
        wq_lo = sb("wq_lo", [P, HALVES, D], F32R)
        wo = sb("wo", [P, HALVES, D])
        wo_hi = sb("wo_hi", [P, HALVES, D], F32R)
        wo_lo = sb("wo_lo", [P, HALVES, D], F32R)
        bq = sb("bq", [P, HALVES])
        bo_rest = sb("bo_rest", [BO_ROWS, D])
        bo_part = [sb(f"bo_part{n}", [BO_ROWS, D], BF16) for n in range(2)]
        bo_rows = sb("bo_rows", [BO_ROWS, D], BF16)
        gate = sb("gate", [P, 2])
        tgate = sb("tgate", [P, 2])
        scale_in = sb("scale_in", [P, 2])
        sc = sb("sc", [P, 9])
        wf = sb("wf", [P, HALVES, D], BF16)
        wf_8 = sb("wf_8", [P, HALVES, D], FP8)
        wf_8h = sb("wf_8h", [P, HALVES, D], FP8)
        wf_q = sb("wf_q", [P, HALVES, D], BF16)
        bias_b = sb("bias_b", [P, D], BF16)
        ctxT = sb("ctxT", [P, HALVES, B * KEYS])
        kT = sb("kT", [P, HALVES, B * KEYS])
        kT_hi = sb("kT_hi", [P, HALVES, B * KEYS], F32R)
        kT_lo = sb("kT_lo", [P, HALVES, B * KEYS], F32R)
        k_stack = sb("k_stack", [STACK, HALVES, PAIRS_PER_HALF, B * KEYS], F32R)
        minus_half = sb("minus_half", [P, TILES])

        x_all = sb("x_all", [P, B, TILES, D])
        mask_i = [sb(f"mask_i{p}", [P, TILES, KEYS], I32) for p in range(2)]
        mask_ti = [sb(f"mask_ti{p}", [KEYS, S], I32) for p in range(2)]
        kT_twice = sb("kT_twice", [P, HALVES, 2, KEYS])
        stats = sb("stats", [P, TILES, 6])
        mv = sb("mv", [P, TILES, 2])
        vare = sb("vare", [P, TILES])
        rstd = sb("rstd", [P, TILES])
        z = sb("z", [P, TILES, D])
        z_hi = sb("z_hi", [P, HALVES, S], F32R)
        z_lo = sb("z_lo", [P, HALVES, S], F32R)
        flag = sb("flag", [P, S], BF16)
        qf = sb("qf", [P, HALVES, S])
        q_hi = sb("q_hi", [P, HALVES, S], F32R)
        q_lo = sb("q_lo", [P, HALVES, S], F32R)
        q_stack = sb("q_stack", [STACK, HALVES, PAIRS_PER_HALF, S], F32R)
        k_hi = sb("k_hi", [P, HALVES, HPH, KEYS], F32R)
        k_pairs = [sb(f"k_pairs{p}", [STACK, HALVES * PAIRS_PER_HALF, 2, KEYS], F32R) for p in range(2)]
        v_blk = [sb(f"v_blk{p}", [P, D]) for p in range(2)]
        mbias = sb("mbias", [P, TILES, KEYS], BF16)
        shift = [sb(f"shift{p}", [SHIFT_ROWS, S], BF16) for p in range(2)]
        negmax = sb("negmax", [P, TILES, H])
        negmax_b = sb("negmax_b", [P, TILES, 2, H], BF16)

        probs = sb("probs", [P, 2 * GROUPS, S])
        pv = [sb(f"pv{p}", [P, HALVES, S]) for p in range(2)]
        den = sb("den", [P, S])
        rden = sb("rden", [P, TILES * H])
        rden_x = sb("rden_x", [P, TILES, HALVES, P])
        att = sb("att", [P, HALVES, S])
        att_hi = sb("att_hi", [P, HALVES, S], F32R)
        att_lo = sb("att_lo", [P, HALVES, S], F32R)
        wf_f, wf_c = (att[:, m].rearrange("p (k d) -> p k d", k=HALVES) for m in range(2))
        wf_e = pv[1][:, 0].rearrange("p (k d) -> p k d", k=HALVES)
        stats2 = sb("stats2", [P, TILES, 6])
        mv2 = sb("mv2", [P, TILES, 2])
        vare2 = sb("vare2", [P, TILES])
        rstd2 = sb("rstd2", [P, TILES])
        u = sb("u", [P, TILES, D], BF16)
        u8 = sb("u8", [P, HALVES, S], FP8)
        y = sb("y", [P, TILES, D], BF16)
        yb = sb("yb", [P, TILES, D], BF16)

        score = [ctx.enter_context(nc.psum_tensor(f"score{s}", [P, 2 * S], F32)) for s in range(2)]
        pv_ps = ctx.enter_context(nc.psum_tensor("pv_ps", [P, S], F32))
        den_ps = ctx.enter_context(nc.psum_tensor("den_ps", [P, S], F32))
        front_ps = ctx.enter_context(nc.psum_tensor("front_ps", [P, S], F32))
        rear_ps = ctx.enter_context(nc.psum_tensor("rear_ps", [P, S], F32))
        front_b = front_ps[:, :].bitcast(BF16)
        rear_b = rear_ps[:, :].bitcast(BF16)

        last_den, last_rden, last_wo = front_ps[:, :], (score[0][:, 0:S], score[0][:, S:2 * S]), (score[1][:, 0:S], score[1][:, S:2 * S])
        last_att, last_att_hi, last_att_lo = qf, z_hi, z_lo
        last_u, last_y = (pv_ps[:, :].bitcast(BF16), rear_b), (den_ps[:, :], front_ps[:, :])

        wq_loaded = sem("wq_loaded")
        ctx_loaded = sem("ctx_loaded")
        c_loaded = sem("c_loaded")
        w_loaded = sem("w_loaded")
        x_loaded = [sem(f"x_loaded{b}") for b in range(3)]
        x_rest_loaded = sem("x_rest_loaded")
        m_loaded = [sem(f"m_loaded{p}") for p in range(2)]
        wqhi_ready = sem("wqhi_ready")
        wqlo_ready = sem("wqlo_ready")
        wohi_ready = sem("wohi_ready")
        wolo_ready = sem("wolo_ready")
        tanh_ready = sem("tanh_ready")
        half_ready = sem("half_ready")
        bo_step = sem("bo_step")
        bo_ready = sem("bo_ready")
        scales_ready = sem("scales_ready")
        wfq_ready = sem("wfq_ready")
        wf_step = sem("wf_step")
        kt_done = sem("kt_done")
        kt_ready = sem("kt_ready")
        kthi_ready = sem("kthi_ready")
        ktlo_ready = sem("ktlo_ready")
        k_staged = sem("k_staged")
        q_staged = sem("q_staged")
        stats_done = sem("stats_done")
        mv_done = sem("mv_done")
        vare_done = sem("vare_done")
        rstd_done = sem("rstd_done")
        z_ready = sem("z_ready")
        zt_done = sem("zt_done")
        zhi_ready = sem("zhi_ready")
        zlo_ready = sem("zlo_ready")
        mb_ready = sem("mb_ready")
        mt_ready = sem("mt_ready")
        masked_counted = sem("masked_counted")
        flag_ready = sem("flag_ready")
        q_done = sem("q_done")
        qf_ready = sem("qf_ready")
        qhi_ready = sem("qhi_ready")
        qlo_ready = sem("qlo_ready")
        khi_ready = sem("khi_ready")
        kpairs_ready = sem("kpairs_ready")
        kv_ready = sem("kv_ready")
        v_done = sem("v_done")
        vblk_ready = sem("vblk_ready")
        a_done = sem("a_done")
        max_done = sem("max_done")
        nmhi_ready = sem("nmhi_ready")
        nm_ready = sem("nm_ready")
        nmt_done = sem("nmt_done")
        shift_ready = sem("shift_ready")
        b_done = sem("b_done")
        exp_done = sem("exp_done")
        pv_done = sem("pv_done")
        pv_copied = sem("pv_copied")
        den_copied = sem("den_copied")
        dent_done = sem("dent_done")
        rden_ready = sem("rden_ready")
        rdenx_ready = sem("rdenx_ready")
        rdent_done = sem("rdent_done")
        att_ready = sem("att_ready")
        atthi_ready = sem("atthi_ready")
        attlo_ready = sem("attlo_ready")
        wo_done = sem("wo_done")
        x1_ready = sem("x1_ready")
        stats2_done = sem("stats2_done")
        mv2_done = sem("mv2_done")
        vare2_done = sem("vare2_done")
        rstd2_done = sem("rstd2_done")
        u_ready = sem("u_ready")
        ut_done = sem("ut_done")
        u8_ready = sem("u8_ready")
        y_done = sem("y_done")
        y_ready = sem("y_ready")
        yb_ready = sem("yb_ready")
        out_ready = sem("out_ready")
        stored = sem("stored")

        C_LOADS = 3
        W_LOADS = 7


        def wait(eng, s, n):
            if not (isinstance(n, int) and n <= 0):
                eng.wait_ge(s, n)

        def wait_all(eng, first, *rest):
            rest = [(s, n) for s, n in rest if not (isinstance(n, int) and n <= 0)]
            for _, n in rest:
                if not isinstance(n, int):
                    eng.compute_val(n)
            eng.wait_ge(*first)
            for s, n in rest:
                eng.wait_ge(s, n)

        def all_iterations(eng, iteration):
            def plain(i):
                iteration(i, i % 2, ahead=i + 2 < B, front=0 <= i + 1 < B, current=0 <= i < B, rear=0 <= i - 1 < B,
                          tail=i - 2 >= 0)

            for i in range(-2, 2):
                plain(i)
            with eng.Fori(0, (B - 4) // 2) as k:
                for h in range(2):
                    iteration(2 * k + (2 + h), h, ahead=True, front=True, current=True, rear=True, tail=True)
            for i in range(B - 2, B):
                plain(i)

        def masks_of(b, p):
            return 32 * ((b - p) // 2 + 1) if isinstance(b, int) else 16 * (b - p) + 32

        block = ctx.enter_context(nc.Block())

        @block.sync
        def _(sp):
            def batch_loads(b, p):
                sp.dma_start(mask_i[p][:], mask[b].rearrange("a (t p) j -> p (a t) j", p=P)).then_inc(m_loaded[p], 16)
                sp.dma_start(mask_ti[p][:], mask_t[b].rearrange("a j s -> j (a s)")).then_inc(m_loaded[p], 16)

            def stack(dst, parts, staged, ready=(None, None, None)):
                for n, part in enumerate(parts):
                    if ready[n] is not None:
                        sp.wait_ge(ready[n], 1)
                    for j in range(PAIRS_PER_HALF):
                        sp.dma_start(dst[PAIR * n:PAIR * (n + 1), :, j].bitcast(F32),
                                     part[PAIR * j:PAIR * (j + 1)].bitcast(F32)).then_inc(staged, 16)

            def stack_q(f):
                wait(sp, b_done, 4 * f)
                wait(sp, qhi_ready, 2 * f + 2)
                wait(sp, qlo_ready, 2 * f + 2)
                stack(q_stack, (q_hi, q_lo, q_hi), q_staged)

            def next_loads(b, k, p):
                wait_all(sp, (c_loaded, 16 * C_LOADS), (m_loaded[p], 32 * k), (mb_ready, b - 1), (mt_ready, b - 1))
                batch_loads(bass.ds(b, 1), p)

            sp.dma_start(x_all[:, 0], x[0].rearrange("(t p) d -> p t d", p=P)).then_inc(x_loaded[0], 16)
            sp.dma_start(wq[:], wq_t.rearrange("(k p) n -> p k n", p=P)).then_inc(wq_loaded, 16)
            sp.dma_start(ctxT[:], ctx_t.rearrange("(k p) n -> p k n", p=P)).then_inc(ctx_loaded, 16)
            sp.dma_start(cf[:], const_f32).then_inc(c_loaded, 16)
            sp.dma_start(bq[:], bq_col).then_inc(c_loaded, 16)
            sp.dma_start(cb[:], const_b16).then_inc(c_loaded, 16)
            batch_loads(bass.ds(0, 1), 0)
            sp.dma_start(gate[:], gates.broadcast_to((P, 2))).then_inc(w_loaded, 16)
            sp.dma_start(bo_rest[:], bo_row.broadcast_to((BO_ROWS, D))).then_inc(w_loaded, 16)
            sp.dma_start(wo[:], wo_t.rearrange("(k p) n -> p k n", p=P)).then_inc(w_loaded, 16)
            sp.dma_start(x_all[:, 1], x[1].rearrange("(t p) d -> p t d", p=P)).then_inc(x_loaded[1], 16)
            batch_loads(bass.ds(1, 1), 1)
            sp.dma_start(wf[:], w_ffn.rearrange("(k p) n -> p k n", p=P)).then_inc(w_loaded, 16)
            sp.dma_start(scale_in[:, 0:1], s_in.broadcast_to((P, 1))).then_inc(w_loaded, 16)
            sp.dma_start(scale_in[:, 1:2], s_k.broadcast_to((P, 1))).then_inc(w_loaded, 16)
            sp.dma_start(bias_b[:], bias_row.broadcast_to((P, D))).then_inc(w_loaded, 16)
            stack(k_stack, (kT_hi, kT_hi, kT_lo), k_staged, (kthi_ready, None, ktlo_ready))

            def iteration(i, half, h, load):
                stack_q(i + 1)
                if isinstance(i, int) and i == -1:
                    sp.dma_start(x_all[:, 2], x[2].rearrange("(t p) d -> p t d", p=P)).then_inc(x_loaded[2], 16)
                    sp.dma_start(x_all[:, 3:B], x[3:B].rearrange("b (t p) d -> p b t d", p=P)).then_inc(x_rest_loaded, 16)
                if load:
                    next_loads(i + 3, half + 1, h)

            iteration(-1, 0, 0, load=True)
            iteration(0, 0, 1, load=True)
            with sp.Fori(0, (B - 4) // 2) as k:
                for h in range(2):
                    iteration(2 * k + (1 + h), k + 1, h, load=True)
            for i in range(B - 3, B - 1):
                iteration(i, None, None, load=False)

            sp.wait_ge(out_ready, 2 * B - 2)
            sp.dma_start(out[B - 2].rearrange("(t p) d -> p t d", p=P), x_all[:, B - 2]).then_inc(stored, 16)
            for h in range(2):
                sp.wait_ge(out_ready, 2 * B - 1 + h)
                sp.dma_start(out[B - 1, 2 * h * P:2 * (h + 1) * P].rearrange("(t p) d -> p t d", p=P),
                             x_all[:, B - 1, 2 * h:2 * h + 2]).then_inc(stored, 16)
            sp.wait_ge(stored, 16 * (B + 1))

        @block.gpsimd
        def _(pool):
            pool.memset(minus_half[:], -0.5)
            pool.memset(bo_rows[:], 0.0).then_inc(half_ready, 1)
            pool.wait_ge(half_ready, 1)

            def mask_bias(f, p):
                wait_all(pool, (half_ready, 1), (m_loaded[p], masks_of(f, p)),
                         (a_done, 4 * f))
                pool.tensor_scalar(mbias[:], mask_i[p][:], 0.0, MASKED, ALU.is_equal, ALU.mult).then_inc(mb_ready, 1)

            def mask_bias_by_key(e, p):
                wait_all(pool, (half_ready, 1), (m_loaded[p], masks_of(e, p)),
                         (b_done, 4 * e - 4))
                pool.tensor_scalar(shift[p][0:KEYS, :], mask_ti[p][:], 0.0, MASKED, ALU.is_equal,
                                   ALU.mult).then_inc(mt_ready, 1)

            def inverse_deviation(b, agg, first, result, first_done, result_done, agg_done, free):
                wait_all(pool, (half_ready, 1), (agg_done, b + 1),
                         (free, b))
                pool.tensor_scalar(first[:], agg[:, :, 1], EPS, None, ALU.add).then_inc(first_done, 1)
                wait(pool, first_done, b + 1)
                pool.tensor_tensor(result[:], first[:], minus_half[:], ALU.pow).then_inc(result_done, 1)

            def block_keys(f):
                if isinstance(f, int) and f == 0:
                    wait(pool, kt_ready, 2)
                wait(pool, a_done, 4 * f)
                shape = (P, HPH, KEYS)
                for m in range(HALVES):
                    ins = pool.tensor_tensor(k_hi[:, m],
                                             kT[:, m, bass.ds(f * KEYS, KEYS)].unsqueeze(1).broadcast_to(shape),
                                             own_head.unsqueeze(2).broadcast_to(shape), ALU.mult)
                ins.then_inc(khi_ready, 1)

            def q_low(f, m):
                wait(pool, qhi_ready, 2 * f + m + 1)
                wait(pool, q_staged, STAGED * f)
                pool.tensor_tensor(q_lo[:, m], qf[:, m], q_hi[:, m].bitcast(F32), ALU.subtract).then_inc(qlo_ready, 1)

            def att_low(r, m):
                wait(pool, atthi_ready, 2 * r + m + 1)
                pool.tensor_tensor(att_lo[:, m], att[:, m], att_hi[:, m].bitcast(F32), ALU.subtract).then_inc(attlo_ready, 1)

            def split_bo():
                pool.wait_ge(w_loaded, 16 * W_LOADS)
                for n in range(2):
                    pool.tensor_copy(bo_part[n][:], bo_rest[:]).then_inc(bo_step, 1)
                    pool.wait_ge(bo_step, 2 * n + 1)
                    pool.tensor_tensor(bo_rest[:], bo_rest[:], bo_part[n][:], ALU.subtract).then_inc(bo_step, 1)
                    pool.wait_ge(bo_step, 2 * n + 2)
                for n, part in enumerate((bo_part[0], bo_part[1], bo_rest)):
                    pool.tensor_copy(bo_rows[32 * n:32 * n + 1], part[32 * n:32 * n + 1]).then_inc(bo_ready, 1)
                    pool.wait_ge(bo_ready, n + 1)

            def iteration(i, pc, ahead, front, current, rear, tail):
                is_first = isinstance(i, int) and i == -2
                is_second = isinstance(i, int) and i == -1
                is_third = isinstance(i, int) and i == 0
                later = ahead and not (isinstance(i, int) and i == -2)
                is_last = isinstance(i, int) and i == B - 1
                inner_rear = rear and not is_last
                inner_front = front and not is_second
                f, r, e, t = i + 1, i - 1, i + 2, i - 2
                pf = 1 - pc
                if tail:
                    inverse_deviation(t, mv2, vare2, rstd2, vare2_done, rstd2_done, mv2_done, u_ready)
                if front:
                    block_keys(f)
                    mask_bias(f, pf)
                if is_third:
                    split_bo()
                if is_first:
                    inverse_deviation(e, mv, vare, rstd, vare_done, rstd_done, mv_done, z_ready)
                if front:
                    q_low(f, 0)
                if later:
                    inverse_deviation(e, mv, vare, rstd, vare_done, rstd_done, mv_done, z_ready)
                if front:
                    q_low(f, 1)
                if ahead:
                    mask_bias_by_key(e, pc)
                if rear:
                    att_low(r, 0)
                    att_low(r, 1)

            all_iterations(pool, iteration)

            inverse_deviation(B - 2, mv2, vare2, rstd2, vare2_done, rstd2_done, mv2_done, u_ready)
            for h in range(2):
                half = slice(2 * h, 2 * h + 2)
                pool.wait_ge(mv_done, B + h + 1)
                pool.tensor_scalar(vare[:, half], mv[:, half, 1], EPS, None, ALU.add).then_inc(vare_done, 1)
                pool.wait_ge(vare_done, B + h + 1)
                pool.tensor_tensor(rstd[:, half], vare[:, half], minus_half[:, half], ALU.pow).then_inc(rstd_done, 1)

        @block.scalar
        def _(act):
            act.wait_ge(wq_loaded, 16)
            nc.scalar.activation(wq_hi[:], wq[:], ACT.Copy).then_inc(wqhi_ready, 1)

            def key_high():
                act.wait_ge(kt_ready, 2)
                nc.scalar.activation(kT_hi[:], kT[:], ACT.Copy).then_inc(kthi_ready, 1)

            def z_high(f, m):
                wait(act, zt_done, 2 * f + m + 1)
                wait(act, q_done, 2 * f)
                nc.scalar.activation(z_hi[:, m], front_ps[:, :], ACT.Copy).then_inc(zhi_ready, 1)

            def q_high(f, m):
                wait(act, qf_ready, 2 * f + m + 1)
                wait(act, q_staged, STAGED * f)
                wait(act, a_done, 4 * f)
                nc.scalar.activation(q_hi[:, m], qf[:, m], ACT.Copy).then_inc(qhi_ready, 1)

            def exp(c, g):
                wait(act, b_done, 4 * c + g + 1)
                wait(act, pv_done, 4 * c + g - 3)
                nc.scalar.activation(probs[:, 2 * g:2 * g + 2], score[g % 2][:, :].rearrange("p (a s) -> p a s", a=2),
                                     ACT.Exp, scale=float(DK) ** -0.5).then_inc(exp_done, 1)

            def keys_twice(f):
                if isinstance(f, int) and f == 0:
                    act.wait_ge(kt_ready, 2)
                wait(act, v_done, f)
                nc.scalar.activation(kT_twice[:], kT[:, :, bass.ds(f * KEYS, KEYS)].unsqueeze(2).broadcast_to(
                    (P, HALVES, 2, KEYS)), ACT.Copy).then_inc(kv_ready, 1)

            def key_pairs(f, p):
                if isinstance(f, int) and f == 0:
                    act.wait_ge(k_staged, STAGED)
                wait(act, b_done, 4 * f - 4)
                for h in range(2):
                    ins = nc.scalar.activation(
                        k_pairs[p][:, :, h],
                        k_stack[:, :, :, bass.ds(f * KEYS, KEYS)].rearrange("p m j n -> p (m j) n").bitcast(F32),
                        ACT.Copy, scale=own_in_pair[:, h:h + 1])
                ins.then_inc(kpairs_ready, 1)

            def den_copy(c):
                wait(act, pv_done, 4 * c + 4)
                wait(act, dent_done, c)
                nc.scalar.activation(den[:], den_ps[:, :], ACT.Copy).then_inc(den_copied, 1)

            def spread_reciprocals(r):
                wait(act, rden_ready, r + 1)
                nc.scalar.activation(rden_x[:].rearrange("p t m (h e) -> p (t m h) e", e=DK),
                                     rden[:].unsqueeze(2).broadcast_to((P, TILES * H, DK)),
                                     ACT.Copy).then_inc(rdenx_ready, 1)

            def u_quantise(t):
                wait_all(act, (scales_ready, 1), (ut_done, t + 1))
                nc.scalar.activation(u8[:], rear_b.rearrange("p (m s) -> p m s", m=HALVES), ACT.Copy,
                                     scale=sc[:, 3:4], saturate=False).then_inc(u8_ready, 1)

            def shift_copy(f, p):
                wait(act, nmt_done, f + 1)
                wait(act, b_done, 4 * f - 4)
                nc.scalar.activation(shift[p][KEYS:SHIFT_ROWS, :], front_b[KEYS:SHIFT_ROWS, 0:S],
                                     ACT.Copy).then_inc(shift_ready, 1)

            def pv_copy(c, p, m):
                wait(act, pv_done, 4 * c + 2 * m + 2)
                wait(act, att_ready, 2 * c - 2)
                nc.scalar.activation(pv[p][:, m], pv_ps[:, :], ACT.Copy).then_inc(pv_copied, 1)

            def att_high(r, m):
                wait(act, att_ready, 2 * r + m + 1)
                nc.scalar.activation(att_hi[:, m], att[:, m], ACT.Copy).then_inc(atthi_ready, 1)

            def store(t):
                wait(act, out_ready, 2 * t + 2)
                act.dma_start(out[bass.ds(t, 1)].rearrange("a (n p) d -> p a n d", p=P),
                              x_all[:, bass.ds(t, 1)]).then_inc(stored, 16)

            def y_scale(t, h):
                wait(act, y_done, 2 * t + h + 1)
                nc.scalar.activation(y[:, 2 * h:2 * h + 2], rear_ps[:, :].rearrange("p (a d) -> p a d", a=2), ACT.Copy,
                                     scale=sc[:, 4:5]).then_inc(y_ready, 1)

            def iteration(i, pc, ahead, front, current, rear, tail):
                is_first = isinstance(i, int) and i == -2
                is_second = isinstance(i, int) and i == -1
                is_third = isinstance(i, int) and i == 0
                later = ahead and not (isinstance(i, int) and i == -2)
                is_last = isinstance(i, int) and i == B - 1
                inner_rear = rear and not is_last
                inner_front = front and not is_second
                c, f, r, t = i, i + 1, i - 1, i - 2
                pf = 1 - pc
                if is_first:
                    z_high(0, 0)
                    z_high(0, 1)
                    key_high()
                if is_second:
                    act.wait_ge(w_loaded, 16 * W_LOADS)
                    nc.scalar.activation(tgate[:], gate[:], ACT.Tanh).then_inc(tanh_ready, 1)
                    nc.scalar.activation(wo_hi[:], wo[:], ACT.Copy).then_inc(wohi_ready, 1)
                if inner_front:
                    z_high(f, 0)
                if current:
                    exp(c, 0)
                    exp(c, 1)
                if inner_front:
                    z_high(f, 1)
                if front:
                    keys_twice(f)
                if rear:
                    spread_reciprocals(r)
                if current:
                    exp(c, 2)
                if tail:
                    u_quantise(t)
                if front:
                    q_high(f, 0)
                if current:
                    pv_copy(c, pc, 0)
                if tail:
                    y_scale(t, 0)
                if current:
                    exp(c, 3)
                if front:
                    q_high(f, 1)
                if tail:
                    y_scale(t, 1)
                if front:
                    key_pairs(f, pf)
                if current:
                    pv_copy(c, pc, 1)
                    den_copy(c)
                if rear:
                    att_high(r, 0)
                    att_high(r, 1)
                if is_last:
                    spread_reciprocals(B - 1)
                if front:
                    shift_copy(f, pf)
                if tail:
                    store(t)

            all_iterations(act, iteration)

            for m in range(HALVES):
                act.wait_ge(att_ready, 2 * B - 1 + m)
                nc.scalar.activation(last_att_hi[:, m], last_att[:, m], ACT.Copy).then_inc(atthi_ready, 1)
            u_quantise(B - 2)
            y_scale(B - 2, 0)
            y_scale(B - 2, 1)
            for h in range(2):
                act.wait_ge(ut_done, B + h)
                nc.scalar.activation(u8[:, :, 2 * h * P:2 * (h + 1) * P],
                                     last_u[h].rearrange("p (m s) -> p m s", m=HALVES)[:, :, 2 * h * P:2 * (h + 1) * P],
                                     ACT.Copy, scale=sc[:, 3:4], saturate=False).then_inc(u8_ready, 1)
                act.wait_ge(y_done, 2 * B - 1 + h)
                act.wait_ge(yb_ready, 2 * B - 2)
                nc.scalar.activation(y[:, 2 * h:2 * h + 2], last_y[h].rearrange("p (a d) -> p a d", a=2), ACT.Copy,
                                     scale=sc[:, 4:5]).then_inc(y_ready, 1)

        @block.vector
        def _(dve):
            def split_weights():
                dve.wait_ge(wqhi_ready, 1)
                nc.vector.tensor_tensor(wq_lo[:], wq[:], wq_hi[:].bitcast(F32), ALU.subtract).then_inc(wqlo_ready, 1)

            def add_key_bias(m):
                if m == 0:
                    dve.wait_ge(c_loaded, 16 * C_LOADS)
                dve.wait_ge(kt_done, m + 1)
                nc.vector.tensor_scalar(kT[:, m], score[0][:, m * S:(m + 1) * S], bq[:, m:m + 1], None,
                                        ALU.add).then_inc(kt_ready, 1)

            def split_keys():
                dve.wait_ge(kthi_ready, 1)
                nc.vector.tensor_tensor(kT_lo[:], kT[:], kT_hi[:].bitcast(F32), ALU.subtract).then_inc(ktlo_ready, 1)

            def prepare_scales():
                dve.wait_ge(tanh_ready, 1)
                dve.wait_ge(wohi_ready, 1)
                nc.vector.tensor_tensor(wo_lo[:], wo[:], wo_hi[:].bitcast(F32), ALU.subtract).then_inc(wolo_ready, 1)
                nc.vector.reciprocal(sc[:, 0:2], scale_in[:]).then_inc(wf_step, 1)
                dve.wait_ge(wf_step, 1)
                nc.vector.tensor_scalar(sc[:, 5:6], sc[:, 0:1], sc[:, 0:1], None, ALU.mult).then_inc(wf_step, 1)
                nc.vector.tensor_scalar(sc[:, 8:9], scale_in[:, 0:1], scale_in[:, 1:2], None, ALU.mult)
                dve.wait_ge(wf_step, 2)
                nc.vector.tensor_scalar(sc[:, 2:3], sc[:, 5:6], FP8_MAX ** 2 / D, None, ALU.is_gt).then_inc(wf_step, 1)
                dve.wait_ge(wf_step, 3)
                nc.vector.tensor_scalar(sc[:, 6:7], sc[:, 2:3], -0.5, 1.0, ALU.mult, ALU.add)
                nc.vector.tensor_scalar(sc[:, 7:8], sc[:, 2:3], 1.0, None, ALU.add).then_inc(wf_step, 1)
                dve.wait_ge(wf_step, 4)
                nc.vector.tensor_scalar(sc[:, 3:4], sc[:, 0:1], sc[:, 6:7], None, ALU.mult)
                nc.vector.tensor_scalar(sc[:, 4:5], sc[:, 8:9], sc[:, 7:8], None, ALU.mult).then_inc(scales_ready, 1)

            def prepare_ffn():
                nc.vector.tensor_scalar(wf_f, wf[:], sc[:, 1:2], None, ALU.mult).then_inc(wf_step, 1)
                dve.wait_ge(wf_step, 5)
                nc.vector.tensor_scalar(wf_c, wf_f, FP8_MAX, -FP8_MAX, ALU.min, ALU.max)
                nc.vector.tensor_scalar(wf_8h[:], wf_f, 0.5, None, ALU.mult, saturate=False).then_inc(wf_step, 1)
                dve.wait_ge(wf_step, 6)
                nc.vector.tensor_copy(wf_8[:], wf_c, saturate=False)
                nc.vector.tensor_scalar(wf_f, wf_8h[:], 2.0, None, ALU.mult).then_inc(wf_step, 1)
                dve.wait_ge(wf_step, 7)
                nc.vector.tensor_scalar(wf_c, wf_8h[:], FP8_MAX / 2, -FP8_MAX / 2, ALU.min, ALU.max).then_inc(wf_step, 1)
                dve.wait_ge(wf_step, 8)
                nc.vector.scalar_tensor_tensor(wf_e.rearrange("p a b -> p (a b)"), wf_c.rearrange("p a b -> p (a b)"),
                                               -2.0, wf_f.rearrange("p a b -> p (a b)"), ALU.mult,
                                               ALU.add).then_inc(wf_step, 1)
                dve.wait_ge(wf_step, 9)
                nc.vector.tensor_tensor(wf_q[:], wf_8[:], wf_e, ALU.add).then_inc(wfq_ready, 1)

            def layer_norm_stats(b, st, agg, first_done, second_done):
                for n in range(TILES):
                    ins = nc.vector.bn_stats(st[:, n], x_all[:, bass.ds(b, 1), n].rearrange("p a d -> p (a d)"))
                ins.then_inc(first_done, 1)
                wait_all(dve, (x_loaded[0], 16), (first_done, b + 1))
                for n in range(TILES):
                    ins = nc.vector.bn_aggr(agg[:, n], st[:, n])
                ins.then_inc(second_done, 1)

            def first_stats(e):
                if isinstance(e, int) and e < 3:
                    dve.wait_ge(x_loaded[e], 16)
                else:
                    dve.wait_ge(x_rest_loaded, 16)
                layer_norm_stats(e, stats, mv, stats_done, mv_done)

            def first_norm(e):
                wait(dve, rstd_done, e + 1)
                wait(dve, zt_done, 2 * e)
                for n in range(TILES):
                    ins = nc.vector.tensor_scalar(z[:, n], x_all[:, bass.ds(e, 1), n].rearrange("p a d -> p (a d)"),
                                                  mv[:, n, 0:1], rstd[:, n:n + 1], ALU.subtract, ALU.mult)
                ins.then_inc(z_ready, 1)

            def unmasked_flag(e, bank):
                wait(dve, masked_counted, e + 1)
                nc.vector.tensor_scalar(flag[:], bank, KEYS * MASKED, None,
                                        ALU.not_equal).then_inc(flag_ready, 1)

            def z_low(f, m):
                wait(dve, zhi_ready, 2 * f + m + 1)
                wait(dve, q_done, 2 * f)
                nc.vector.tensor_tensor(z_lo[:, m], front_ps[:, :], z_hi[:, m].bitcast(F32),
                                        ALU.subtract).then_inc(zlo_ready, 1)

            def q_float(f, m):
                wait(dve, q_done, 2 * f + m + 1)
                wait(dve, flag_ready, f + 1)
                wait(dve, qlo_ready, 2 * f)
                nc.vector.scalar_tensor_tensor(qf[:, m], front_ps[:, :], bq[:, m:m + 1], flag[:], ALU.add,
                                               ALU.mult).then_inc(qf_ready, 1)

            def block_values(f, p):
                wait(dve, v_done, f + 1)
                wait(dve, pv_done, 4 * f - 4)
                nc.vector.tensor_tensor(v_blk[p][:], front_ps[:, 0:D], own_half, ALU.mult).then_inc(vblk_ready, 1)

            def row_max(f, n):
                wait(dve, a_done, 4 * f + n + 1)
                nc.vector.tensor_reduce(negmax[:, n], score[n % 2][:, :].rearrange("p (h j) -> p h j", h=H), AX_X,
                                        ALU.max, negate=True).then_inc(max_done, 1)

            def split_max(f):
                wait(dve, max_done, 4 * f + 4)
                wait(dve, nmt_done, f)
                nc.vector.tensor_copy(negmax_b[:, :, 0], negmax[:]).then_inc(nmhi_ready, 1)
                wait(dve, nmhi_ready, f + 1)
                nc.vector.tensor_tensor(negmax_b[:, :, 1], negmax[:], negmax_b[:, :, 0],
                                        ALU.subtract).then_inc(nm_ready, 1)

            def reciprocals(r, ps):
                wait(dve, dent_done, r + 1)
                src = ps.rearrange("p (t a b m h e) -> p t a b m h e", t=TILES, a=2, b=2, m=2, h=2)
                dst = rden[:].rearrange("p (t m a b h) -> p t m a b h", t=TILES, m=2, a=2, b=2)
                for a in range(2):
                    for m in range(HALVES):
                        ins = nc.vector.reciprocal(dst[:, :, m, a], src[:, :, 1 - a, :, m, :, 0])
                ins.then_inc(rden_ready, 1)

            def attend(r, p, m, ps):
                wait(dve, rdent_done, 2 * r + m + 1)
                nc.vector.tensor_tensor(att[:, m], ps, pv[p][:, m], ALU.mult).then_inc(att_ready, 1)

            def residual(r, h, ps):
                wait(dve, wo_done, 2 * r + h + 1)
                xb = x_all[:, bass.ds(r, 1), 2 * h:2 * h + 2].rearrange("p a t d -> p (a t d)")
                nc.vector.scalar_tensor_tensor(xb, ps, tgate[:, 0:1], xb, ALU.mult,
                                               ALU.add).then_inc(x1_ready, 1)

            def second_norm(t):
                wait(dve, rstd2_done, t + 1)
                for n in range(TILES):
                    ins = nc.vector.tensor_scalar(u[:, n], x_all[:, bass.ds(t, 1), n].rearrange("p a d -> p (a d)"),
                                                  mv2[:, n, 0:1], rstd2[:, n:n + 1], ALU.subtract, ALU.mult)
                ins.then_inc(u_ready, 1)

            def add_bias(t, h):
                wait(dve, y_ready, 2 * t + h + 1)
                nc.vector.tensor_tensor(yb[:, 2 * h:2 * h + 2], y[:, 2 * h:2 * h + 2],
                                        bias_b[:].unsqueeze(1).broadcast_to((P, 2, D)), ALU.add).then_inc(yb_ready, 1)

            def output(t, h):
                wait(dve, yb_ready, 2 * t + h + 1)
                xb = x_all[:, bass.ds(t, 1), 2 * h:2 * h + 2].rearrange("p a t d -> p (a t d)")
                nc.vector.scalar_tensor_tensor(xb, yb[:, 2 * h:2 * h + 2].rearrange("p t d -> p (t d)"), tgate[:, 1:2],
                                               xb, ALU.mult, ALU.add).then_inc(out_ready, 1)

            def iteration(i, pc, ahead, front, current, rear, tail):
                is_first = isinstance(i, int) and i == -2
                is_second = isinstance(i, int) and i == -1
                is_third = isinstance(i, int) and i == 0
                later = ahead and not (isinstance(i, int) and i == -2)
                is_last = isinstance(i, int) and i == B - 1
                inner_rear = rear and not is_last
                inner_front = front and not is_second
                f, r, e, t = i + 1, i - 1, i + 2, i - 2
                pf = 1 - pc
                if is_first:
                    first_stats(e)
                    first_norm(e)
                    split_weights()
                    add_key_bias(0)
                    z_low(0, 0)
                    add_key_bias(1)
                if inner_front:
                    z_low(f, 0)
                if rear:
                    reciprocals(r, rear_ps[:, :])
                if tail:
                    second_norm(t)
                if is_third:
                    prepare_scales()
                    prepare_ffn()
                if front:
                    z_low(f, 1)
                if is_second:
                    split_keys()
                    unmasked_flag(f, den_ps[:, :])
                if front:
                    q_float(f, 0)
                if later:
                    first_stats(e)
                if front:
                    q_float(f, 1)
                if later:
                    first_norm(e)
                if tail:
                    add_bias(t, 0)
                    output(t, 0)
                if rear:
                    attend(r, pf, 0, rear_ps[:, :])
                if front:
                    block_values(f, pf)
                if tail:
                    add_bias(t, 1)
                if rear:
                    attend(r, pf, 1, rear_ps[:, :])
                if tail:
                    output(t, 1)
                if front:
                    row_max(f, 0)
                    row_max(f, 1)
                if later:
                    unmasked_flag(e, front_ps[:, :])
                if front:
                    row_max(f, 2)
                if is_last:
                    reciprocals(B - 1, last_den)
                if rear:
                    residual(r, 0, rear_ps[:, :])
                if front:
                    row_max(f, 3)
                    split_max(f)
                if inner_rear:
                    residual(r, 1, rear_ps[:, :])
                    wait_all(dve, (x_loaded[0], 16), (x1_ready, 2 * r + 2))
                    layer_norm_stats(r, stats2, mv2, stats2_done, mv2_done)

            all_iterations(dve, iteration)

            r = B - 1
            for m in range(HALVES):
                dve.wait_ge(rdent_done, 2 * r + m + 1)
                nc.vector.tensor_tensor(last_att[:, m], last_rden[m], pv[r % 2][:, m], ALU.mult).then_inc(att_ready, 1)
            residual(r - 1, 1, rear_ps[:, :])
            for m in range(HALVES):
                dve.wait_ge(atthi_ready, 2 * r + m + 1)
                nc.vector.tensor_tensor(last_att_lo[:, m], last_att[:, m], last_att_hi[:, m].bitcast(F32),
                                        ALU.subtract).then_inc(attlo_ready, 1)
            dve.wait_ge(x1_ready, 2 * r)
            layer_norm_stats(r - 1, stats2, mv2, stats2_done, mv2_done)
            second_norm(r - 1)
            for h in range(2):
                residual(r, h, last_wo[h])
                dve.wait_ge(x1_ready, 2 * r + h + 1)
                for n in (2 * h, 2 * h + 1):
                    ins = nc.vector.bn_stats(stats[:, n], x_all[:, r, n])
                ins.then_inc(stats_done, 1)
                dve.wait_ge(stats_done, B + h + 1)
                for n in (2 * h, 2 * h + 1):
                    ins = nc.vector.bn_aggr(mv[:, n], stats[:, n])
                ins.then_inc(mv_done, 1)
            for h in range(2):
                dve.wait_ge(rstd_done, B + h + 1)
                dve.wait_ge(ut_done, r)
                for n in (2 * h, 2 * h + 1):
                    ins = nc.vector.tensor_scalar(u[:, n], x_all[:, r, n], mv[:, n, 0:1], rstd[:, n:n + 1],
                                                  ALU.subtract, ALU.mult)
                ins.then_inc(u_ready, 1)
            for b in (r - 1, r):
                for h in range(2):
                    add_bias(b, h)
                    output(b, h)

        @block.tensor
        def _(pe):
            mm = nc.tensor.matmul

            def project_keys(m):
                if m == 0:
                    pe.wait_ge(wq_loaded, 16)
                    pe.wait_ge(ctx_loaded, 16)
                for k in range(HALVES):
                    ins = mm(score[0][:, m * S:(m + 1) * S], wq[:, k, m * P:(m + 1) * P], ctxT[:, k], start=(k == 0),
                             stop=(k == HALVES - 1))
                ins.then_inc(kt_done, 1)

            def count_masked(e, p, bank):
                wait(pe, mt_ready, e + 1)
                if isinstance(e, int) and e == 0:
                    pe.wait_ge(c_loaded, 16 * C_LOADS)
                wait(pe, vblk_ready, e)
                mm(bank, ones_b[0:KEYS], shift[p][0:KEYS], start=True, stop=True).then_inc(masked_counted, 1)

            def z_transpose(f, m):
                wait(pe, z_ready, f + 1)
                if isinstance(f, int) and f == 0 and m == 0:
                    pe.wait_ge(c_loaded, 16 * C_LOADS)
                if m == 0:
                    wait(pe, shift_ready, f)
                else:
                    wait(pe, zlo_ready, 2 * f + 1)
                for t in range(TILES):
                    ins = nc.tensor.transpose(front_ps[:, t * P:(t + 1) * P], z[:, t, m * P:(m + 1) * P], ident)
                ins.then_inc(zt_done, 1)

            def q_project(f, m):
                wait(pe, zlo_ready, 2 * f + 2)
                if m == 1:
                    wait(pe, qf_ready, 2 * f + 1)
                if isinstance(f, int) and f == 0 and m == 0:
                    pe.wait_ge(wqlo_ready, 1)
                steps = [(a, b, k) for k in range(HALVES) for a, b in ((wq_hi, z_hi), (wq_lo, z_hi), (wq_hi, z_lo))]
                for n, (a, b, k) in enumerate(steps):
                    ins = mm(front_ps[:, :], a[:, k, m * P:(m + 1) * P], b[:, k], start=(n == 0),
                             stop=(n == len(steps) - 1))
                ins.then_inc(q_done, 1)

            def v_transpose(f):
                wait(pe, kv_ready, f + 1)
                wait(pe, qf_ready, 2 * f + 2)
                for m in range(HALVES):
                    ins = nc.tensor.transpose(front_ps[:, m * P:(m + 1) * P],
                                              kT_twice[:, m].rearrange("p a j -> p (a j)"), ident)
                ins.then_inc(v_done, 1)

            def scores_by_query(f, p, t):
                wait(pe, qhi_ready, 2 * f + 2)
                wait(pe, khi_ready, f + 1)
                wait(pe, mb_ready, f + 1)
                if t < 2:
                    wait(pe, exp_done, 4 * f - 1 + t)
                    if isinstance(f, int) and f == 0 and t == 0:
                        wait(pe, kt_ready, 2)
                else:
                    wait(pe, max_done, 4 * f + t - 1)
                for m in range(HALVES):
                    dst = score[t % 2][:, m * S:(m + 1) * S]
                    mm(dst, q_hi[:, m, t * P:(t + 1) * P], k_hi[:, m].rearrange("p h j -> p (h j)"), start=True,
                       stop=False)
                    ins = mm(dst, ident_b, mbias[:, t].unsqueeze(1).broadcast_to((P, HPH, KEYS)), start=False, stop=True)
                ins.then_inc(a_done, 1)

            def negmax_transpose(f, ahead):
                wait(pe, nm_ready, f + 1)
                if ahead:
                    wait(pe, flag_ready, f + 2)
                else:
                    wait(pe, vblk_ready, f + 1)
                for t in range(TILES):
                    ins = nc.tensor.transpose(front_b[KEYS:SHIFT_ROWS, t * P:(t + 1) * P],
                                              negmax_b[:, t].rearrange("p a h -> p (a h)"), ident_b)
                ins.then_inc(nmt_done, 1)

            def scores_by_key(c, p, g):
                wait(pe, q_staged, STAGED * (c + 1))
                wait(pe, kpairs_ready, c + 1)
                wait(pe, shift_ready, c + 1)
                if g < 2:
                    wait(pe, max_done, 4 * c + g + 3)
                else:
                    wait(pe, exp_done, 4 * c + g - 1)
                for n in range(2):
                    pair = 2 * g + n
                    m, j = divmod(pair, 4)
                    dst = score[g % 2][:, n * S:(n + 1) * S]
                    mm(dst, k_pairs[p][:, pair].rearrange("p h j -> p (h j)"), q_stack[:, m, j], start=True, stop=False)
                    ins = mm(dst, shift_w[0:SHIFT_ROWS, pair], shift[p][:], start=False, stop=True)
                ins.then_inc(b_done, 1)

            def weigh_values(c, p, g):
                wait(pe, exp_done, 4 * c + g + 1)
                wait(pe, vblk_ready, c + 1)
                if g == 0:
                    wait(pe, den_copied, c)
                if g % 2 == 0:
                    wait(pe, pv_copied, 2 * c + g // 2)
                for n in range(2):
                    pair = 2 * g + n
                    m, j = divmod(pair, 4)
                    mm(pv_ps[32 * j:32 * j + 32, :], v_blk[p][:, 32 * pair:32 * pair + 32], probs[:, pair], start=True,
                       stop=True)
                for n in range(2):
                    pair = 2 * g + n
                    m, j = divmod(pair, 4)
                    jd = (j + 2) % 4
                    ins = mm(den_ps[32 * jd:32 * jd + 32, :], den_w[:, m], probs[:, pair], start=(m == 0), stop=(m == 1))
                ins.then_inc(pv_done, 1)

            def den_transpose(r):
                wait(pe, den_copied, r + 1)
                wait(pe, x1_ready, 2 * r)
                for t in range(TILES):
                    ins = nc.tensor.transpose(rear_ps[:, t * P:(t + 1) * P], den[:, t * P:(t + 1) * P], ident)
                ins.then_inc(dent_done, 1)

            def last_den_transpose():
                pe.wait_ge(den_copied, B)
                pe.wait_ge(shift_ready, B)
                for t in range(TILES):
                    ins = nc.tensor.transpose(last_den[:, t * P:(t + 1) * P], den[:, t * P:(t + 1) * P], ident)
                ins.then_inc(dent_done, 1)

            def rden_transpose(r, m):
                wait(pe, rdenx_ready, r + 1)
                if m == 0:
                    wait(pe, y_ready, 2 * r)
                if m == 1:
                    wait(pe, att_ready, 2 * r + 1)
                for t in range(TILES):
                    ins = nc.tensor.transpose(rear_ps[:, t * P:(t + 1) * P], rden_x[:, t, m], ident)
                ins.then_inc(rdent_done, 1)

            def out_project(r, h, banks=None):
                wait(pe, attlo_ready, 2 * r + 2)
                if isinstance(r, int) and r == 0 and h == 0:
                    pe.wait_ge(wolo_ready, 1)
                    pe.wait_ge(bo_ready, 3)
                if h == 1 and not banks:
                    wait(pe, x1_ready, 2 * r + 1)
                for t in (2 * h, 2 * h + 1):
                    dst = (banks[h] if banks else rear_ps[:, :])[:, (t % 2) * D:(t % 2 + 1) * D]
                    hi, lo = (last_att_hi, last_att_lo) if banks else (att_hi, att_lo)
                    steps = [(a, w, m) for m in range(HALVES) for a, w in ((hi, wo_hi), (lo, wo_hi), (hi, wo_lo))]
                    for n, (a, w, m) in enumerate(steps):
                        mm(dst, a[:, m, t * P:(t + 1) * P], w[:, m], start=(n == 0), stop=False)
                    ins = mm(dst, ones_b[0:BO_ROWS], bo_rows[:], start=False, stop=True)
                ins.then_inc(wo_done, 1)

            def u_transpose(r, rear):
                wait(pe, u_ready, r + 1)
                if rear:
                    wait(pe, rden_ready, r + 2)
                else:
                    wait(pe, x1_ready, 2 * r + 2)
                for m in range(HALVES):
                    for t in range(TILES):
                        ins = nc.tensor.transpose(rear_b[:, m * S + t * P:m * S + (t + 1) * P],
                                                  u[:, t, m * P:(m + 1) * P], ident_b)
                ins.then_inc(ut_done, 1)

            def ffn(r, h):
                if h == 0:
                    wait_all(pe, (wfq_ready, 1), (u8_ready, r + 1))
                else:
                    wait_all(pe, (wfq_ready, 1), (y_ready, 2 * r + 1))
                for t in (2 * h, 2 * h + 1):
                    for m in range(HALVES):
                        ins = mm(rear_ps[:, (t % 2) * D:(t % 2 + 1) * D], u8[:, m, t * P:(t + 1) * P], wf_q[:, m],
                                 start=(m == 0), stop=(m == HALVES - 1))
                ins.then_inc(y_done, 1)

            def iteration(i, pc, ahead, front, current, rear, tail):
                is_first = isinstance(i, int) and i == -2
                is_second = isinstance(i, int) and i == -1
                is_third = isinstance(i, int) and i == 0
                later = ahead and not (isinstance(i, int) and i == -2)
                is_last = isinstance(i, int) and i == B - 1
                inner_rear = rear and not is_last
                inner_front = front and not is_second
                c, f, r, e, t = i, i + 1, i - 1, i + 2, i - 2
                pf = 1 - pc
                if is_first:
                    project_keys(0)
                    z_transpose(0, 0)
                    project_keys(1)
                if inner_front:
                    z_transpose(f, 0)
                if current:
                    scores_by_key(c, pc, 0)
                if rear:
                    den_transpose(r)
                if current:
                    scores_by_key(c, pc, 1)
                if front:
                    z_transpose(f, 1)
                if current:
                    weigh_values(c, pc, 0)
                    scores_by_key(c, pc, 2)
                if tail:
                    u_transpose(t, rear)
                if front:
                    q_project(f, 0)
                if current:
                    weigh_values(c, pc, 1)
                if tail:
                    ffn(t, 0)
                if current:
                    scores_by_key(c, pc, 3)
                if front:
                    q_project(f, 1)
                if tail:
                    ffn(t, 1)
                if current:
                    weigh_values(c, pc, 2)
                if front:
                    v_transpose(f)
                if rear:
                    rden_transpose(r, 0)
                if current:
                    weigh_values(c, pc, 3)
                if rear:
                    rden_transpose(r, 1)
                if front:
                    scores_by_query(f, pf, 0)
                    scores_by_query(f, pf, 1)
                if is_first:
                    count_masked(e, pc, den_ps[:, :])
                if later:
                    count_masked(e, pc, front_ps[:, :])
                if front:
                    scores_by_query(f, pf, 2)
                if is_last:
                    last_den_transpose()
                if rear:
                    out_project(r, 0)
                if front:
                    scores_by_query(f, pf, 3)
                if inner_rear:
                    out_project(r, 1)
                if front:
                    negmax_transpose(f, ahead)

            all_iterations(pe, iteration)

            r = B - 1
            pe.wait_ge(rdenx_ready, B)
            pe.wait_ge(exp_done, 4 * B - 1)
            for m in range(HALVES):
                for t in range(TILES):
                    ins = nc.tensor.transpose(last_rden[m][:, t * P:(t + 1) * P], rden_x[:, t, m], ident)
                ins.then_inc(rdent_done, 1)
            out_project(r - 1, 1)
            pe.wait_ge(exp_done, 4 * B)
            out_project(r, 0, last_wo)
            out_project(r, 1, last_wo)
            u_transpose(r - 1, False)
            ffn(r - 1, 0)
            ffn(r - 1, 1)
            pe.wait_ge(pv_copied, 2 * B)
            pe.wait_ge(y_ready, 2 * B - 2)
            for h in range(2):
                pe.wait_ge(u_ready, B + h)
                for m in range(HALVES):
                    for t in (2 * h, 2 * h + 1):
                        ins = nc.tensor.transpose(last_u[h][:, m * S + t * P:m * S + (t + 1) * P],
                                                  u[:, t, m * P:(m + 1) * P], ident_b)
                ins.then_inc(ut_done, 1)
            for h in range(2):
                pe.wait_ge(u8_ready, B + h)
                pe.wait_ge(rden_ready, B)
                for t in (2 * h, 2 * h + 1):
                    for m in range(HALVES):
                        ins = mm(last_y[h][:, (t % 2) * D:(t % 2 + 1) * D], u8[:, m, t * P:(t + 1) * P], wf_q[:, m],
                                 start=(m == 0), stop=(m == HALVES - 1))
                ins.then_inc(y_done, 1)


_INS = ["x", "mask", "mask_t", "ctx_t", "wq_t", "bq_col", "wo_t", "bo_row", "gates", "w_ffn", "s_in",
        "s_k", "bias_row", "const_f32", "const_b16"]


def kernel(**inputs):
    import numpy as _np
    import concourse.bacc as _bacc
    from concourse import mybir as _mybir
    from concourse.bass_utils import run_bass_kernel_spmd as _run

    given = {k: _np.asarray(v) for k, v in inputs.items()}
    x, keys = given["x"], given["ctx_1024"]
    batch, seq, dim = x.shape
    n_keys = keys.shape[1]
    mask = given["mask_Bx1xSxS2_if1"].reshape(batch, seq, n_keys)
    f32, b16 = constants(dim, 16, n_keys)
    keys_t = keys.transpose(0, 2, 1)
    laid = {
        "x": x,
        "mask": mask,
        "mask_t": mask.transpose(0, 2, 1),
        "ctx_t": keys_t.transpose(1, 0, 2).reshape(dim, batch * n_keys),
        "wq_t": given["L0_xattn_Wq"].T,
        "bq_col": given["L0_xattn_bq"].reshape(dim // 128, 128).T,
        "wo_t": given["L0_xattn_Wo"].T,
        "bo_row": given["L0_xattn_bo"].reshape(1, dim),
        "gates": _np.concatenate([given["g_xattn"], given["g_ffn"]]).reshape(1, 2),
        "w_ffn": given["L0_ffn_kernel"],
        "s_in": given["L0_ffn_input_scale"].reshape(1, 1),
        "s_k": given["L0_ffn_kernel_scale"].reshape(1, 1),
        "bias_row": given["L0_ffn_bias"].reshape(1, dim),
        "const_f32": f32,
        "const_b16": b16.astype(given["L0_ffn_bias"].dtype),
    }
    nc = _bacc.Bacc("TRN2", target_bir_lowering=False, num_devices=1)
    arrays, args = {}, []
    for name in _INS:
        a = _np.ascontiguousarray(laid[name])
        arrays[f"in_{name}_dram"] = a
        args.append(nc.dram_tensor(f"in_{name}_dram", a.shape, _mybir.dt.from_np(a.dtype), kind="ExternalInput").ap())
    args.append(nc.dram_tensor("out_0_dram", x.shape, _mybir.dt.from_np(x.dtype), kind="ExternalOutput").ap())
    build(nc, *args)
    return _run(nc, [arrays], core_ids=[0]).results[0]["out_0_dram"]
```

```python
from contextlib import ExitStack

import numpy as np

import concourse.bass as bass
from concourse import mybir

ALU = mybir.AluOpType
ACT = mybir.ActivationFunctionType
AX_X = mybir.AxisListType.X
F32 = mybir.dt.float32
F32R = mybir.dt.float32r
BF16 = mybir.dt.bfloat16
FP8 = mybir.dt.float8e4
I32 = mybir.dt.int32

P = 128
MASKED = -(2.0 ** 100)
EPS = 1e-5
FP8_MAX = 240.0


def constants(D, H, KEYS):
    DK = D // H
    row = np.arange(P)
    pairs = H // 2
    ident = np.eye(P, dtype=np.float32)
    own_head = (row[:, None] // DK == np.arange(P // DK)[None, :]).astype(np.float32)
    den = np.zeros((P, 2, 2, 2, 8), np.float32)
    for m in range(2):
        for hh in range(2):
            den[hh * KEYS:(hh + 1) * KEYS, m, m, hh, :] = 1.0
    own_in_pair = ((row[:, None] // DK) % 2 == np.arange(2)[None, :]).astype(np.float32)
    own_key_half = (row[:, None] // KEYS == np.arange(2)[None, :]).astype(np.float32)
    f32 = np.concatenate([ident, own_head, own_key_half, den.reshape(P, 64), own_in_pair], 1)
    shift = np.zeros((P, pairs, 2, KEYS), np.float32)
    for p in range(pairs):
        for hh in range(2):
            shift[np.arange(KEYS), p, hh, np.arange(KEYS)] = 1.0
            shift[KEYS + 2 * p + hh, p, hh, :] = 1.0
            shift[KEYS + H + 2 * p + hh, p, hh, :] = 1.0
    b16 = np.concatenate([ident, shift.reshape(P, -1), np.ones((P, P), np.float32)], 1)
    return np.ascontiguousarray(f32), np.ascontiguousarray(b16)


def build(nc, x, mask, mask_t, ctx_t, wq_t, bq_col, wo_t, bo_row, gates, w_ffn, s_in, s_k, bias_row,
          const_f32, const_b16, out):
    B, S, D = x.shape
    KEYS = mask.shape[2]
    H = 16
    DK = D // H
    TILES = S // P
    HALVES = D // P
    HPH = P // DK
    GROUPS = 4
    SHIFT_ROWS = KEYS + 2 * H
    PAIR = 2 * DK
    STACK = 3 * PAIR
    PAIRS_PER_HALF = P // PAIR
    STAGED = 16 * 3 * PAIRS_PER_HALF
    assert (S, D, KEYS, DK, HALVES) == (512, 256, 64, 16, 2) and B % 2 == 0

    with ExitStack() as ctx:
        def sb(name, shape, dt=F32):
            return ctx.enter_context(nc.sbuf_tensor(name, shape, dt))

        def sem(name):
            return ctx.enter_context(nc.semaphore(name))

        widths = (P, HPH, 2, 64, 2)
        cf = sb("cf", [P, sum(widths)])
        ident, own_head, own_key_half, den_w, own_in_pair = (
            cf[:, sum(widths[:n]):sum(widths[:n + 1])] for n in range(len(widths)))
        den_w = den_w.rearrange("p (m c) -> p m c", m=2)
        own_in_pair = own_in_pair[0:STACK]
        cb = sb("cb", [P, P + 8 * P + P], BF16)
        ident_b = cb[:, 0:P]
        shift_w = cb[:, P:9 * P].rearrange("p (g c) -> p g c", g=8)
        ones_b = cb[:, 9 * P:10 * P]
        wq = sb("wq", [P, HALVES, D])
        wq_hi = sb("wq_hi", [P, HALVES, D], F32R)
        wq_lo = sb("wq_lo", [P, HALVES, D], F32R)
        wo = sb("wo", [P, HALVES, D])
        wo_hi = sb("wo_hi", [P, HALVES, D], F32R)
        wo_lo = sb("wo_lo", [P, HALVES, D], F32R)
        bq = sb("bq", [P, HALVES])
        bo_tg = sb("bo_tg", [P, D])
        gate = sb("gate", [P, 2])
        tgate = sb("tgate", [P, 2])
        scale_in = sb("scale_in", [P, 2])
        sc = sb("sc", [P, 9])
        wf = sb("wf", [P, HALVES, D], BF16)
        wf_8 = sb("wf_8", [P, HALVES, D], FP8)
        wf_8h = sb("wf_8h", [P, HALVES, D], FP8)
        wf_q = sb("wf_q", [P, HALVES, D], BF16)
        bias_b = sb("bias_b", [P, D], BF16)
        ctxT = sb("ctxT", [P, HALVES, B * KEYS])
        kT = sb("kT", [P, HALVES, B * KEYS])
        kT_hi = sb("kT_hi", [P, HALVES, B * KEYS], F32R)
        kT_lo = sb("kT_lo", [P, HALVES, B * KEYS], F32R)
        k_stack = sb("k_stack", [STACK, HALVES, PAIRS_PER_HALF, B * KEYS], F32R)
        minus_half = sb("minus_half", [P, TILES])

        x_all = sb("x_all", [P, B, TILES, D])
        mask_i = [sb(f"mask_i{p}", [P, TILES, KEYS], I32) for p in range(2)]
        mask_ti = [sb(f"mask_ti{p}", [KEYS, S], I32) for p in range(2)]
        kT_twice = sb("kT_twice", [P, HALVES, 2, KEYS])
        stats = sb("stats", [P, TILES, 6])
        mv = sb("mv", [P, TILES, 2])
        vare = sb("vare", [P, TILES])
        rstd = sb("rstd", [P, TILES])
        z = sb("z", [P, TILES, D])
        z_hi = sb("z_hi", [P, HALVES, S], F32R)
        z_lo = sb("z_lo", [P, HALVES, S], F32R)
        flag = sb("flag", [P, S], BF16)
        qf = sb("qf", [P, HALVES, S])
        q_hi = sb("q_hi", [P, HALVES, S], F32R)
        q_lo = sb("q_lo", [P, HALVES, S], F32R)
        q_stack = sb("q_stack", [STACK, HALVES, PAIRS_PER_HALF, S], F32R)
        k_hi = sb("k_hi", [P, HALVES, HPH, KEYS], F32R)
        k_pairs = [sb(f"k_pairs{p}", [STACK, HALVES * PAIRS_PER_HALF, 2, KEYS], F32R) for p in range(2)]
        v_blk = [sb(f"v_blk{p}", [P, D]) for p in range(2)]
        mbias = sb("mbias", [P, TILES, KEYS], BF16)
        shift = [sb(f"shift{p}", [SHIFT_ROWS, S], BF16) for p in range(2)]
        negmax = sb("negmax", [P, TILES, H])
        negmax_b = sb("negmax_b", [P, TILES, 2, H], BF16)

        probs = sb("probs", [P, 2 * GROUPS, S])
        pv = [sb(f"pv{p}", [P, HALVES, S]) for p in range(2)]
        den = sb("den", [P, S])
        rden = sb("rden", [P, TILES * H])
        rden_x = sb("rden_x", [P, TILES, HALVES, P])
        att = sb("att", [P, HALVES, S])
        att_hi = sb("att_hi", [P, HALVES, S], F32R)
        att_lo = sb("att_lo", [P, HALVES, S], F32R)
        wf_f, wf_c = (att[:, m].rearrange("p (k d) -> p k d", k=HALVES) for m in range(2))
        wf_e = pv[1][:, 0].rearrange("p (k d) -> p k d", k=HALVES)
        stats2 = sb("stats2", [P, TILES, 6])
        mv2 = sb("mv2", [P, TILES, 2])
        vare2 = sb("vare2", [P, TILES])
        rstd2 = sb("rstd2", [P, TILES])
        u = sb("u", [P, TILES, D], BF16)
        u8 = sb("u8", [P, HALVES, S], FP8)
        y = sb("y", [P, TILES, D], BF16)
        yb = sb("yb", [P, TILES, D], BF16)
        gated_y = sb("gated_y", [P, TILES, D])

        score = [ctx.enter_context(nc.psum_tensor(f"score{s}", [P, 2 * S], F32)) for s in range(2)]
        pv_ps = ctx.enter_context(nc.psum_tensor("pv_ps", [P, S], F32))
        den_ps = ctx.enter_context(nc.psum_tensor("den_ps", [P, S], F32))
        front_ps = ctx.enter_context(nc.psum_tensor("front_ps", [P, S], F32))
        rear_ps = ctx.enter_context(nc.psum_tensor("rear_ps", [P, S], F32))
        den_b = den_ps[:, :].bitcast(BF16)
        rear_b = rear_ps[:, :].bitcast(BF16)

        last_den = front_ps[:, :]
        last_rden, last_wo = ((score[s][:, 0:S], score[s][:, S:2 * S]) for s in range(2))
        last_att, last_att_hi, last_att_lo = qf, z_hi, z_lo
        last_ut, last_ffn = (pv_ps[:, :].bitcast(BF16), rear_b), (den_ps[:, :], front_ps[:, :])
        last_u = z[:].bitcast(BF16)[:, :, 0:D]
        last_u8 = sb("last_u8", [P, HALVES, S], FP8)
        last_y = sb("last_y", [P, TILES, D], BF16)
        last_yb = sb("last_yb", [P, TILES, D], BF16)

        wq_loaded = sem("wq_loaded")
        ctx_loaded = sem("ctx_loaded")
        c_loaded = sem("c_loaded")
        w_loaded = sem("w_loaded")
        x_loaded = [sem(f"x_loaded{b}") for b in range(3)]
        x_rest_loaded = sem("x_rest_loaded")
        m_loaded = [sem(f"m_loaded{p}") for p in range(2)]
        wqhi_ready = sem("wqhi_ready")
        wqlo_ready = sem("wqlo_ready")
        wohi_ready = sem("wohi_ready")
        wolo_ready = sem("wolo_ready")
        tanh_ready = sem("tanh_ready")
        half_ready = sem("half_ready")
        botg_ready = sem("botg_ready")
        xres_ready = sem("xres_ready")
        scales_ready = sem("scales_ready")
        wfq_ready = sem("wfq_ready")
        wf_step = sem("wf_step")
        kt_done = sem("kt_done")
        kt_ready = sem("kt_ready")
        kthi_ready = sem("kthi_ready")
        ktlo_ready = sem("ktlo_ready")
        k_staged = sem("k_staged")
        q_staged = sem("q_staged")
        stats_done = sem("stats_done")
        mv_done = sem("mv_done")
        vare_done = sem("vare_done")
        rstd_done = sem("rstd_done")
        z_ready = sem("z_ready")
        zt_done = sem("zt_done")
        zhi_ready = sem("zhi_ready")
        zlo_ready = sem("zlo_ready")
        mb_ready = sem("mb_ready")
        mt_ready = sem("mt_ready")
        masked_counted = sem("masked_counted")
        flag_ready = sem("flag_ready")
        q_done = sem("q_done")
        qf_ready = sem("qf_ready")
        qhi_ready = sem("qhi_ready")
        qlo_ready = sem("qlo_ready")
        khi_ready = sem("khi_ready")
        kpairs_ready = sem("kpairs_ready")
        kv_ready = sem("kv_ready")
        v_done = sem("v_done")
        vblk_ready = sem("vblk_ready")
        a_done = sem("a_done")
        max_done = sem("max_done")
        nmhi_ready = sem("nmhi_ready")
        nm_ready = sem("nm_ready")
        nmt_done = sem("nmt_done")
        shift_ready = sem("shift_ready")
        b_done = sem("b_done")
        exp_done = sem("exp_done")
        pv_done = sem("pv_done")
        pv_copied = sem("pv_copied")
        den_copied = sem("den_copied")
        dent_done = sem("dent_done")
        rden_ready = sem("rden_ready")
        rdenx_ready = sem("rdenx_ready")
        rdent_done = sem("rdent_done")
        att_ready = sem("att_ready")
        atthi_ready = sem("atthi_ready")
        attlo_ready = sem("attlo_ready")
        wo_done = sem("wo_done")
        x1_ready = sem("x1_ready")
        stats2_done = sem("stats2_done")
        mv2_done = sem("mv2_done")
        vare2_done = sem("vare2_done")
        rstd2_done = sem("rstd2_done")
        u_ready = sem("u_ready")
        ut_done = sem("ut_done")
        u8_ready = sem("u8_ready")
        y_done = sem("y_done")
        y_ready = sem("y_ready")
        yb_ready = sem("yb_ready")
        gated_ready = sem("gated_ready")
        out_ready = sem("out_ready")
        stored = sem("stored")
        (last_rdent_done, last_att_ready, last_atthi_ready, last_attlo_ready, last_wo_done, last_x1_ready,
         last_stats_done, last_mv_done, last_vare_done, last_rstd_done, last_u_ready, last_ut_done, last_u8_ready,
         last_ffn_done, last_y_ready, last_yb_ready, last_out_ready) = (sem("last_" + name) for name in (
             "rdent_done", "att_ready", "atthi_ready", "attlo_ready", "wo_done", "x1_ready", "stats_done", "mv_done",
             "vare_done", "rstd_done", "u_ready", "ut_done", "u8_ready", "ffn_done", "y_ready", "yb_ready",
             "out_ready"))

        C_LOADS = 3
        W_LOADS = 7

        def wait(eng, s, n):
            if not (isinstance(n, int) and n <= 0):
                eng.wait_ge(s, n)

        def wait_all(eng, first, *rest):
            rest = [(s, n) for s, n in rest if not (isinstance(n, int) and n <= 0)]
            for _, n in rest:
                if not isinstance(n, int):
                    eng.compute_val(n)
            eng.wait_ge(*first)
            for s, n in rest:
                eng.wait_ge(s, n)

        def all_iterations(eng, iteration):
            def plain(i):
                iteration(i, i % 2, ahead=i + 2 < B, front=0 <= i + 1 < B, current=0 <= i < B, rear=0 <= i - 1 < B,
                          tail=i - 2 >= 0)

            for i in range(-2, 2):
                plain(i)
            with eng.Fori(0, (B - 4) // 2) as k:
                for h in range(2):
                    iteration(2 * k + (2 + h), h, ahead=True, front=True, current=True, rear=True, tail=True)
            for i in range(B - 2, B):
                plain(i)

        def masks_of(b, p):
            return 32 * ((b - p) // 2 + 1) if isinstance(b, int) else 16 * (b - p) + 32

        block = ctx.enter_context(nc.Block())

        @block.sync
        def _(sp):
            def batch_loads(b, p):
                sp.dma_start(mask_i[p][:], mask[b].rearrange("a (t p) j -> p (a t) j", p=P)).then_inc(m_loaded[p], 16)
                sp.dma_start(mask_ti[p][:], mask_t[b].rearrange("a j s -> j (a s)")).then_inc(m_loaded[p], 16)

            def stack(dst, rows, part, staged):
                for n in rows:
                    for j in range(PAIRS_PER_HALF):
                        sp.dma_start(dst[PAIR * n:PAIR * (n + 1), :, j].bitcast(F32),
                                     part[PAIR * j:PAIR * (j + 1)].bitcast(F32)).then_inc(staged, 16)

            def stack_q(f):
                wait(sp, b_done, 4 * f)
                wait(sp, qhi_ready, 2 * f + 2)
                stack(q_stack, (0, 2), q_hi, q_staged)
                wait(sp, qlo_ready, 2 * f + 2)
                stack(q_stack, (1,), q_lo, q_staged)

            def next_loads(b, k, p):
                wait_all(sp, (c_loaded, 16 * C_LOADS), (m_loaded[p], 32 * k), (mb_ready, b - 1), (mt_ready, b - 1))
                batch_loads(bass.ds(b, 1), p)

            sp.dma_start(x_all[:, 0], x[0].rearrange("(t p) d -> p t d", p=P)).then_inc(x_loaded[0], 16)
            sp.dma_start(wq[:], wq_t.rearrange("(k p) n -> p k n", p=P)).then_inc(wq_loaded, 16)
            sp.dma_start(ctxT[:], ctx_t.rearrange("(k p) n -> p k n", p=P)).then_inc(ctx_loaded, 16)
            sp.dma_start(cf[:], const_f32).then_inc(c_loaded, 16)
            sp.dma_start(bq[:], bq_col).then_inc(c_loaded, 16)
            sp.dma_start(cb[:], const_b16).then_inc(c_loaded, 16)
            batch_loads(bass.ds(0, 1), 0)
            sp.dma_start(gate[:], gates.broadcast_to((P, 2))).then_inc(w_loaded, 16)
            sp.dma_start(bo_tg[:], bo_row.broadcast_to((P, D))).then_inc(w_loaded, 16)
            sp.dma_start(wo[:], wo_t.rearrange("(k p) n -> p k n", p=P)).then_inc(w_loaded, 16)
            sp.dma_start(x_all[:, 1], x[1].rearrange("(t p) d -> p t d", p=P)).then_inc(x_loaded[1], 16)
            batch_loads(bass.ds(1, 1), 1)
            sp.dma_start(wf[:], w_ffn.rearrange("(k p) n -> p k n", p=P)).then_inc(w_loaded, 16)
            sp.dma_start(scale_in[:, 0:1], s_in.broadcast_to((P, 1))).then_inc(w_loaded, 16)
            sp.dma_start(scale_in[:, 1:2], s_k.broadcast_to((P, 1))).then_inc(w_loaded, 16)
            sp.dma_start(bias_b[:], bias_row.broadcast_to((P, D))).then_inc(w_loaded, 16)
            sp.wait_ge(kthi_ready, 1)
            stack(k_stack, (0, 1), kT_hi, k_staged)
            sp.wait_ge(ktlo_ready, 1)
            stack(k_stack, (2,), kT_lo, k_staged)

            def iteration(i, half, h, load):
                stack_q(i + 1)
                if isinstance(i, int) and i == -1:
                    sp.dma_start(x_all[:, 2], x[2].rearrange("(t p) d -> p t d", p=P)).then_inc(x_loaded[2], 16)
                    sp.dma_start(x_all[:, 3:B], x[3:B].rearrange("b (t p) d -> p b t d", p=P)).then_inc(x_rest_loaded, 16)
                if load:
                    next_loads(i + 3, half + 1, h)

            iteration(-1, 0, 0, load=True)
            iteration(0, 0, 1, load=True)
            with sp.Fori(0, (B - 4) // 2) as k:
                for h in range(2):
                    iteration(2 * k + (1 + h), k + 1, h, load=True)
            for i in range(B - 3, B - 1):
                iteration(i, None, None, load=False)

            sp.wait_ge(out_ready, 2 * B)
            sp.dma_start(out[B - 2].rearrange("(t p) d -> p t d", p=P), x_all[:, B - 2]).then_inc(stored, 16)
            for h in range(2):
                sp.wait_ge(last_out_ready, h + 1)
                sp.dma_start(out[B - 1, 2 * h * P:2 * (h + 1) * P].rearrange("(t p) d -> p t d", p=P),
                             x_all[:, B - 1, 2 * h:2 * h + 2]).then_inc(stored, 16)
            sp.wait_ge(stored, 16 * (B + 1))

        @block.gpsimd
        def _(pool):
            pool.memset(minus_half[:, 0:2], -0.5).then_inc(out_ready, 1)
            pool.memset(minus_half[:, 2:3], -0.5).then_inc(out_ready, 1)
            pool.memset(minus_half[:, 3:4], -0.5).then_inc(half_ready, 1)
            pool.wait_ge(half_ready, 1)

            def mask_bias(f, p):
                wait_all(pool, (half_ready, 1), (m_loaded[p], masks_of(f, p)),
                         (a_done, 4 * f))
                pool.tensor_scalar(mbias[:], mask_i[p][:], 0.0, MASKED, ALU.is_equal, ALU.mult).then_inc(mb_ready, 1)

            def mask_bias_by_key(e, p):
                wait_all(pool, (half_ready, 1), (m_loaded[p], masks_of(e, p)),
                         (b_done, 4 * e - 4))
                pool.tensor_scalar(shift[p][0:KEYS, :], mask_ti[p][:], 0.0, MASKED, ALU.is_equal,
                                   ALU.mult).then_inc(mt_ready, 1)

            def inverse_deviation(b, agg, first, result, first_done, result_done, agg_done):
                wait_all(pool, (half_ready, 1), (agg_done, b + 1))
                pool.tensor_scalar(first[:], agg[:, :, 1], EPS, None, ALU.add).then_inc(first_done, 1)
                wait(pool, first_done, b + 1)
                pool.tensor_tensor(result[:], first[:], minus_half[:], ALU.pow).then_inc(result_done, 1)

            def block_keys(f):
                if isinstance(f, int) and f == 0:
                    wait(pool, kt_ready, 2)
                wait(pool, a_done, 4 * f)
                shape = (P, HPH, KEYS)
                for m in range(HALVES):
                    ins = pool.tensor_tensor(k_hi[:, m],
                                             kT[:, m, bass.ds(f * KEYS, KEYS)].unsqueeze(1).broadcast_to(shape),
                                             own_head.unsqueeze(2).broadcast_to(shape), ALU.mult)
                ins.then_inc(khi_ready, 1)

            def q_low(f, m):
                wait(pool, qhi_ready, 2 * f + m + 1)
                wait(pool, q_staged, STAGED * f)
                pool.tensor_tensor(q_lo[:, m], qf[:, m], q_hi[:, m].bitcast(F32), ALU.subtract).then_inc(qlo_ready, 1)

            def att_low(r, m):
                wait(pool, atthi_ready, 2 * r + m + 1)
                pool.tensor_tensor(att_lo[:, m], att[:, m], att_hi[:, m].bitcast(F32), ALU.subtract).then_inc(attlo_ready, 1)

            def gate_output_bias():
                pool.wait_ge(w_loaded, 16 * W_LOADS)
                pool.wait_ge(tanh_ready, 1)
                pool.tensor_scalar(bo_tg[:], bo_tg[:], tgate[:, 0:1], None, ALU.mult).then_inc(botg_ready, 1)
                pool.wait_ge(botg_ready, 1)

            def add_output_bias(f):
                wait(pool, z_ready, f + 1)
                xb = x_all[:, bass.ds(f, 1)].rearrange("p a t d -> p (a t) d")
                pool.tensor_tensor(xb, xb, bo_tg[:].unsqueeze(1).broadcast_to((P, TILES, D)),
                                   ALU.add).then_inc(xres_ready, 1)

            def last_inverse_deviation(h):
                half = slice(2 * h, 2 * h + 2)
                pool.wait_ge(last_mv_done, h + 1)
                pool.tensor_scalar(vare[:, half], mv[:, half, 1], EPS, None, ALU.add).then_inc(last_vare_done, 1)
                pool.wait_ge(last_vare_done, h + 1)
                pool.tensor_tensor(rstd[:, half], vare[:, half], minus_half[:, half], ALU.pow).then_inc(last_rstd_done, 1)

            def output(t, h):
                wait(pool, gated_ready, 2 * t + h + 1)
                xb = x_all[:, bass.ds(t, 1), 2 * h:2 * h + 2].rearrange("p a t d -> p (a t) d")
                pool.tensor_tensor(xb, xb, gated_y[:, 2 * h:2 * h + 2], ALU.add).then_inc(out_ready, 1)

            def iteration(i, pc, ahead, front, current, rear, tail):
                is_first = isinstance(i, int) and i == -2
                is_second = isinstance(i, int) and i == -1
                later = ahead and not is_first
                after_second = later and not is_second
                f, r, e, t = i + 1, i - 1, i + 2, i - 2
                pf = 1 - pc
                if tail:
                    inverse_deviation(t, mv2, vare2, rstd2, vare2_done, rstd2_done, mv2_done)
                if is_second:
                    inverse_deviation(e, mv, vare, rstd, vare_done, rstd_done, mv_done)
                if front:
                    block_keys(f)
                if after_second:
                    inverse_deviation(e, mv, vare, rstd, vare_done, rstd_done, mv_done)
                if front:
                    mask_bias(f, pf)
                if is_first:
                    inverse_deviation(e, mv, vare, rstd, vare_done, rstd_done, mv_done)
                if ahead:
                    mask_bias_by_key(e, pc)
                if front:
                    q_low(f, 0)
                    q_low(f, 1)
                if rear:
                    att_low(r, 0)
                    att_low(r, 1)
                if is_second:
                    gate_output_bias()
                if tail:
                    output(t, 0)
                    output(t, 1)
                if front:
                    add_output_bias(f)

            all_iterations(pool, iteration)

            inverse_deviation(B - 2, mv2, vare2, rstd2, vare2_done, rstd2_done, mv2_done)
            last_inverse_deviation(0)
            last_inverse_deviation(1)
            output(B - 2, 0)
            output(B - 2, 1)

        @block.scalar
        def _(act):
            act.wait_ge(wq_loaded, 16)
            nc.scalar.activation(wq_hi[:], wq[:], ACT.Copy).then_inc(wqhi_ready, 1)

            def key_high():
                act.wait_ge(kt_ready, 2)
                nc.scalar.activation(kT_hi[:], kT[:], ACT.Copy).then_inc(kthi_ready, 1)

            def z_high(f, m):
                wait(act, zt_done, 2 * f + m + 1)
                wait(act, q_done, 2 * f)
                nc.scalar.activation(z_hi[:, m], front_ps[:, :], ACT.Copy).then_inc(zhi_ready, 1)

            def q_high(f, m):
                wait(act, qf_ready, 2 * f + m + 1)
                wait(act, q_staged, STAGED * f)
                wait(act, a_done, 4 * f)
                nc.scalar.activation(q_hi[:, m], qf[:, m], ACT.Copy).then_inc(qhi_ready, 1)

            def exp(c, g):
                wait(act, b_done, 4 * c + g + 1)
                wait(act, pv_done, 4 * c + g - 3)
                nc.scalar.activation(probs[:, 2 * g:2 * g + 2], score[g % 2][:, :].rearrange("p (a s) -> p a s", a=2),
                                     ACT.Exp, scale=float(DK) ** -0.5).then_inc(exp_done, 1)

            def keys_twice(f):
                if isinstance(f, int) and f == 0:
                    act.wait_ge(kt_ready, 2)
                wait(act, v_done, f)
                nc.scalar.activation(kT_twice[:], kT[:, :, bass.ds(f * KEYS, KEYS)].unsqueeze(2).broadcast_to(
                    (P, HALVES, 2, KEYS)), ACT.Copy).then_inc(kv_ready, 1)

            def key_pairs(f, p):
                if isinstance(f, int) and f == 0:
                    act.wait_ge(k_staged, STAGED)
                wait(act, b_done, 4 * f - 4)
                for h in range(2):
                    ins = nc.scalar.activation(
                        k_pairs[p][:, :, h],
                        k_stack[:, :, :, bass.ds(f * KEYS, KEYS)].rearrange("p m j n -> p (m j) n").bitcast(F32),
                        ACT.Copy, scale=own_in_pair[:, h:h + 1])
                ins.then_inc(kpairs_ready, 1)

            def den_copy(c):
                wait(act, pv_done, 4 * c + 4)
                wait(act, dent_done, c)
                nc.scalar.activation(den[:], den_ps[:, :], ACT.Copy).then_inc(den_copied, 1)

            def spread_reciprocals(r):
                wait(act, rden_ready, r + 1)
                nc.scalar.activation(rden_x[:].rearrange("p t m (h e) -> p (t m h) e", e=DK),
                                     rden[:].unsqueeze(2).broadcast_to((P, TILES * H, DK)),
                                     ACT.Copy).then_inc(rdenx_ready, 1)

            def u_quantise(t):
                wait_all(act, (scales_ready, 1), (ut_done, t + 1))
                nc.scalar.activation(u8[:], rear_b.rearrange("p (m s) -> p m s", m=HALVES), ACT.Copy,
                                     scale=sc[:, 3:4], saturate=False).then_inc(u8_ready, 1)

            def shift_copy(f, p):
                wait(act, nmt_done, f + 1)
                wait(act, b_done, 4 * f - 4)
                nc.scalar.activation(shift[p][KEYS:SHIFT_ROWS, :], den_b[KEYS:SHIFT_ROWS, 0:S],
                                     ACT.Copy).then_inc(shift_ready, 1)

            def pv_copy(c, p, m):
                wait(act, pv_done, 4 * c + 2 * m + 2)
                wait(act, att_ready, 2 * c - 2)
                nc.scalar.activation(pv[p][:, m], pv_ps[:, :], ACT.Copy).then_inc(pv_copied, 1)

            def att_high(r, m):
                wait(act, att_ready, 2 * r + m + 1)
                nc.scalar.activation(att_hi[:, m], att[:, m], ACT.Copy).then_inc(atthi_ready, 1)

            def store(t):
                wait(act, out_ready, 2 * t + 4)
                act.dma_start(out[bass.ds(t, 1)].rearrange("a (n p) d -> p a n d", p=P),
                              x_all[:, bass.ds(t, 1)]).then_inc(stored, 16)

            def y_scale(t, h):
                wait(act, y_done, 2 * t + h + 1)
                nc.scalar.activation(y[:, 2 * h:2 * h + 2], rear_ps[:, :].rearrange("p (a d) -> p a d", a=2), ACT.Copy,
                                     scale=sc[:, 4:5]).then_inc(y_ready, 1)

            def last_att_high(m):
                act.wait_ge(last_att_ready, m + 1)
                nc.scalar.activation(last_att_hi[:, m], last_att[:, m], ACT.Copy).then_inc(last_atthi_ready, 1)

            def last_u_quantise(h):
                half = slice(2 * h * P, 2 * (h + 1) * P)
                act.wait_ge(last_ut_done, h + 1)
                nc.scalar.activation(last_u8[:, :, half], last_ut[h].rearrange("p (m s) -> p m s", m=HALVES)[:, :, half],
                                     ACT.Copy, scale=sc[:, 3:4], saturate=False).then_inc(last_u8_ready, 1)

            def last_y_scale(h):
                act.wait_ge(last_ffn_done, h + 1)
                nc.scalar.activation(last_y[:, 2 * h:2 * h + 2], last_ffn[h].rearrange("p (a d) -> p a d", a=2), ACT.Copy,
                                     scale=sc[:, 4:5]).then_inc(last_y_ready, 1)

            def gates():
                act.wait_ge(w_loaded, 16 * W_LOADS)
                nc.scalar.activation(tgate[:], gate[:], ACT.Tanh).then_inc(tanh_ready, 1)

            def output_weights_high():
                act.wait_ge(w_loaded, 16 * W_LOADS)
                nc.scalar.activation(wo_hi[:], wo[:], ACT.Copy).then_inc(wohi_ready, 1)

            def block_values(f, p):
                wait(act, v_done, f + 1)
                wait(act, pv_done, 4 * f - 4)
                for h in range(2):
                    ins = nc.scalar.activation(v_blk[p][:].rearrange("p (g a d) -> p g a d", a=2, d=DK)[:, :, h],
                                               front_ps[:, 0:D].rearrange("p (g a d) -> p g a d", a=2, d=DK)[:, :, h],
                                               ACT.Copy, scale=own_key_half[:, h:h + 1])
                ins.then_inc(vblk_ready, 1)

            def gate_y(t, h):
                wait(act, yb_ready, 2 * t + h + 1)
                wait(act, out_ready, 2 * t + h + 1)
                nc.scalar.activation(gated_y[:, 2 * h:2 * h + 2], yb[:, 2 * h:2 * h + 2], ACT.Copy,
                                     scale=tgate[:, 1:2]).then_inc(gated_ready, 1)

            def iteration(i, pc, ahead, front, current, rear, tail):
                is_first = isinstance(i, int) and i == -2
                is_second = isinstance(i, int) and i == -1
                is_last = isinstance(i, int) and i == B - 1
                inner_current = current and not is_last
                inner_front = front and not is_second
                c, f, r, t = i, i + 1, i - 1, i - 2
                pf = 1 - pc
                if is_first:
                    z_high(0, 0)
                if inner_front:
                    z_high(f, 0)
                if is_first:
                    key_high()
                    z_high(0, 1)
                if current:
                    exp(c, 0)
                    exp(c, 1)
                if inner_front:
                    z_high(f, 1)
                if current:
                    exp(c, 2)
                if rear:
                    spread_reciprocals(r)
                if front:
                    keys_twice(f)
                if is_second:
                    output_weights_high()
                if tail:
                    u_quantise(t)
                if current:
                    pv_copy(c, pc, 0)
                if is_second:
                    gates()
                if front:
                    q_high(f, 0)
                if tail:
                    y_scale(t, 0)
                if current:
                    exp(c, 3)
                if tail:
                    y_scale(t, 1)
                if front:
                    q_high(f, 1)
                if rear:
                    att_high(r, 0)
                if is_last:
                    den_copy(c)
                if front:
                    block_values(f, pf)
                if rear:
                    att_high(r, 1)
                if tail:
                    gate_y(t, 0)
                if front:
                    key_pairs(f, pf)
                if tail:
                    gate_y(t, 1)
                if current:
                    pv_copy(c, pc, 1)
                if inner_current:
                    den_copy(c)
                if is_last:
                    spread_reciprocals(B - 1)
                if front:
                    shift_copy(f, pf)
                if tail:
                    store(t)

            all_iterations(act, iteration)

            last_att_high(0)
            last_att_high(1)
            u_quantise(B - 2)
            y_scale(B - 2, 0)
            y_scale(B - 2, 1)
            gate_y(B - 2, 0)
            last_u_quantise(0)
            gate_y(B - 2, 1)
            last_u_quantise(1)
            last_y_scale(0)
            last_y_scale(1)

        @block.vector
        def _(dve):
            def split_weights():
                dve.wait_ge(wqhi_ready, 1)
                nc.vector.tensor_tensor(wq_lo[:], wq[:], wq_hi[:].bitcast(F32), ALU.subtract).then_inc(wqlo_ready, 1)

            def add_key_bias(m):
                if m == 0:
                    dve.wait_ge(c_loaded, 16 * C_LOADS)
                dve.wait_ge(kt_done, m + 1)
                nc.vector.tensor_scalar(kT[:, m], score[0][:, m * S:(m + 1) * S], bq[:, m:m + 1], None,
                                        ALU.add).then_inc(kt_ready, 1)

            def split_keys():
                dve.wait_ge(kthi_ready, 1)
                nc.vector.tensor_tensor(kT_lo[:], kT[:], kT_hi[:].bitcast(F32), ALU.subtract).then_inc(ktlo_ready, 1)

            def prepare_scales():
                dve.wait_ge(tanh_ready, 1)
                dve.wait_ge(wohi_ready, 1)
                nc.vector.tensor_tensor(wo_lo[:], wo[:], wo_hi[:].bitcast(F32), ALU.subtract).then_inc(wolo_ready, 1)
                nc.vector.reciprocal(sc[:, 0:2], scale_in[:]).then_inc(wf_step, 1)
                dve.wait_ge(wf_step, 1)
                nc.vector.tensor_scalar(sc[:, 5:6], sc[:, 0:1], sc[:, 0:1], None, ALU.mult).then_inc(wf_step, 1)
                nc.vector.tensor_scalar(sc[:, 8:9], scale_in[:, 0:1], scale_in[:, 1:2], None, ALU.mult)
                dve.wait_ge(wf_step, 2)
                nc.vector.tensor_scalar(sc[:, 2:3], sc[:, 5:6], FP8_MAX ** 2 / D, None, ALU.is_gt).then_inc(wf_step, 1)
                dve.wait_ge(wf_step, 3)
                nc.vector.tensor_scalar(sc[:, 6:7], sc[:, 2:3], -0.5, 1.0, ALU.mult, ALU.add)
                nc.vector.tensor_scalar(sc[:, 7:8], sc[:, 2:3], 1.0, None, ALU.add).then_inc(wf_step, 1)
                dve.wait_ge(wf_step, 4)
                nc.vector.tensor_scalar(sc[:, 3:4], sc[:, 0:1], sc[:, 6:7], None, ALU.mult)
                nc.vector.tensor_scalar(sc[:, 4:5], sc[:, 8:9], sc[:, 7:8], None, ALU.mult).then_inc(scales_ready, 1)

            def prepare_ffn():
                nc.vector.tensor_scalar(wf_f, wf[:], sc[:, 1:2], None, ALU.mult).then_inc(wf_step, 1)
                dve.wait_ge(wf_step, 5)
                nc.vector.tensor_scalar(wf_c, wf_f, FP8_MAX, -FP8_MAX, ALU.min, ALU.max)
                nc.vector.tensor_scalar(wf_8h[:], wf_f, 0.5, None, ALU.mult, saturate=False).then_inc(wf_step, 1)
                dve.wait_ge(wf_step, 6)
                nc.vector.tensor_copy(wf_8[:], wf_c, saturate=False)
                nc.vector.tensor_scalar(wf_f, wf_8h[:], 2.0, None, ALU.mult).then_inc(wf_step, 1)
                dve.wait_ge(wf_step, 7)
                nc.vector.tensor_scalar(wf_c, wf_8h[:], FP8_MAX / 2, -FP8_MAX / 2, ALU.min, ALU.max).then_inc(wf_step, 1)
                dve.wait_ge(wf_step, 8)
                nc.vector.scalar_tensor_tensor(wf_e.rearrange("p a b -> p (a b)"), wf_c.rearrange("p a b -> p (a b)"),
                                               -2.0, wf_f.rearrange("p a b -> p (a b)"), ALU.mult,
                                               ALU.add).then_inc(wf_step, 1)
                dve.wait_ge(wf_step, 9)
                nc.vector.tensor_tensor(wf_q[:], wf_8[:], wf_e, ALU.add).then_inc(wfq_ready, 1)

            def layer_norm_stats(b, st, agg, first_done, second_done):
                for n in range(TILES):
                    ins = nc.vector.bn_stats(st[:, n], x_all[:, bass.ds(b, 1), n].rearrange("p a d -> p (a d)"))
                ins.then_inc(first_done, 1)
                wait_all(dve, (x_loaded[0], 16), (first_done, b + 1))
                for n in range(TILES):
                    ins = nc.vector.bn_aggr(agg[:, n], st[:, n])
                ins.then_inc(second_done, 1)

            def first_stats(e):
                if isinstance(e, int) and e < 3:
                    dve.wait_ge(x_loaded[e], 16)
                else:
                    dve.wait_ge(x_rest_loaded, 16)
                layer_norm_stats(e, stats, mv, stats_done, mv_done)

            def first_norm(e):
                wait(dve, rstd_done, e + 1)
                wait(dve, zt_done, 2 * e)
                for n in range(TILES):
                    ins = nc.vector.tensor_scalar(z[:, n], x_all[:, bass.ds(e, 1), n].rearrange("p a d -> p (a d)"),
                                                  mv[:, n, 0:1], rstd[:, n:n + 1], ALU.subtract, ALU.mult)
                ins.then_inc(z_ready, 1)

            def unmasked_flag(e, bank):
                wait(dve, masked_counted, e + 1)
                nc.vector.tensor_scalar(flag[:], bank, KEYS * MASKED, None,
                                        ALU.not_equal).then_inc(flag_ready, 1)

            def z_low(f, m):
                wait(dve, zhi_ready, 2 * f + m + 1)
                wait(dve, q_done, 2 * f)
                nc.vector.tensor_tensor(z_lo[:, m], front_ps[:, :], z_hi[:, m].bitcast(F32),
                                        ALU.subtract).then_inc(zlo_ready, 1)

            def q_float(f, m):
                wait(dve, q_done, 2 * f + m + 1)
                wait(dve, flag_ready, f + 1)
                wait(dve, qlo_ready, 2 * f)
                nc.vector.scalar_tensor_tensor(qf[:, m], front_ps[:, :], bq[:, m:m + 1], flag[:], ALU.add,
                                               ALU.mult).then_inc(qf_ready, 1)

            def row_max(f, n):
                wait(dve, a_done, 4 * f + n + 1)
                nc.vector.tensor_reduce(negmax[:, n], score[n % 2][:, :].rearrange("p (h j) -> p h j", h=H), AX_X,
                                        ALU.max, negate=True).then_inc(max_done, 1)

            def split_max(f):
                wait(dve, max_done, 4 * f + 4)
                wait(dve, nmt_done, f)
                nc.vector.tensor_copy(negmax_b[:, :, 0], negmax[:]).then_inc(nmhi_ready, 1)
                wait(dve, nmhi_ready, f + 1)
                nc.vector.tensor_tensor(negmax_b[:, :, 1], negmax[:], negmax_b[:, :, 0],
                                        ALU.subtract).then_inc(nm_ready, 1)

            def reciprocals(r, ps):
                wait(dve, dent_done, r + 1)
                src = ps.rearrange("p (t a b m h e) -> p t a b m h e", t=TILES, a=2, b=2, m=2, h=2)
                dst = rden[:].rearrange("p (t m a b h) -> p t m a b h", t=TILES, m=2, a=2, b=2)
                for a in range(2):
                    for m in range(HALVES):
                        ins = nc.vector.reciprocal(dst[:, :, m, a], src[:, :, 1 - a, :, m, :, 0])
                ins.then_inc(rden_ready, 1)

            def attend(r, p, m, ps):
                wait(dve, rdent_done, 2 * r + m + 1)
                nc.vector.tensor_tensor(att[:, m], ps, pv[p][:, m], ALU.mult).then_inc(att_ready, 1)

            def residual(r, h, ps):
                wait(dve, wo_done, 2 * r + h + 1)
                wait(dve, xres_ready, r + 1)
                xb = x_all[:, bass.ds(r, 1), 2 * h:2 * h + 2].rearrange("p a t d -> p (a t d)")
                nc.vector.scalar_tensor_tensor(xb, ps, tgate[:, 0:1], xb, ALU.mult,
                                               ALU.add).then_inc(x1_ready, 1)

            def second_norm(t):
                wait(dve, rstd2_done, t + 1)
                for n in range(TILES):
                    ins = nc.vector.tensor_scalar(u[:, n], x_all[:, bass.ds(t, 1), n].rearrange("p a d -> p (a d)"),
                                                  mv2[:, n, 0:1], rstd2[:, n:n + 1], ALU.subtract, ALU.mult)
                ins.then_inc(u_ready, 1)

            def add_bias(t, h):
                wait(dve, y_ready, 2 * t + h + 1)
                nc.vector.tensor_tensor(yb[:, 2 * h:2 * h + 2], y[:, 2 * h:2 * h + 2],
                                        bias_b[:].unsqueeze(1).broadcast_to((P, 2, D)), ALU.add).then_inc(yb_ready, 1)

            def last_attend(m):
                dve.wait_ge(last_rdent_done, m + 1)
                nc.vector.tensor_tensor(last_att[:, m], last_rden[m], pv[(B - 1) % 2][:, m],
                                        ALU.mult).then_inc(last_att_ready, 1)

            def last_att_low(m):
                dve.wait_ge(last_atthi_ready, m + 1)
                nc.vector.tensor_tensor(last_att_lo[:, m], last_att[:, m], last_att_hi[:, m].bitcast(F32),
                                        ALU.subtract).then_inc(last_attlo_ready, 1)

            def last_residual(h):
                dve.wait_ge(last_wo_done, h + 1)
                dve.wait_ge(xres_ready, B)
                xb = x_all[:, B - 1, 2 * h:2 * h + 2].rearrange("p t d -> p (t d)")
                nc.vector.scalar_tensor_tensor(xb, last_wo[h], tgate[:, 0:1], xb, ALU.mult,
                                               ALU.add).then_inc(last_x1_ready, 1)

            def last_norm_stats(h):
                dve.wait_ge(last_x1_ready, h + 1)
                for n in (2 * h, 2 * h + 1):
                    ins = nc.vector.bn_stats(stats[:, n], x_all[:, B - 1, n])
                ins.then_inc(last_stats_done, 1)
                dve.wait_ge(last_stats_done, h + 1)
                for n in (2 * h, 2 * h + 1):
                    ins = nc.vector.bn_aggr(mv[:, n], stats[:, n])
                ins.then_inc(last_mv_done, 1)

            def last_second_norm(h):
                dve.wait_ge(last_rstd_done, h + 1)
                for n in (2 * h, 2 * h + 1):
                    ins = nc.vector.tensor_scalar(last_u[:, n], x_all[:, B - 1, n], mv[:, n, 0:1], rstd[:, n:n + 1],
                                                  ALU.subtract, ALU.mult)
                ins.then_inc(last_u_ready, 1)

            def last_add_bias(h):
                dve.wait_ge(last_y_ready, h + 1)
                nc.vector.tensor_tensor(last_yb[:, 2 * h:2 * h + 2], last_y[:, 2 * h:2 * h + 2],
                                        bias_b[:].unsqueeze(1).broadcast_to((P, 2, D)),
                                        ALU.add).then_inc(last_yb_ready, 1)

            def last_output(h):
                dve.wait_ge(last_yb_ready, h + 1)
                xb = x_all[:, B - 1, 2 * h:2 * h + 2].rearrange("p t d -> p (t d)")
                nc.vector.scalar_tensor_tensor(xb, last_yb[:, 2 * h:2 * h + 2].rearrange("p t d -> p (t d)"),
                                               tgate[:, 1:2], xb, ALU.mult, ALU.add).then_inc(last_out_ready, 1)

            def second_stats(t):
                wait_all(dve, (x_loaded[0], 16), (x1_ready, 2 * t + 2))
                layer_norm_stats(t, stats2, mv2, stats2_done, mv2_done)

            def iteration(i, pc, ahead, front, current, rear, tail):
                is_first = isinstance(i, int) and i == -2
                is_second = isinstance(i, int) and i == -1
                is_third = isinstance(i, int) and i == 0
                later = ahead and not is_first
                after_second = later and not is_second
                is_last = isinstance(i, int) and i == B - 1
                inner_rear = rear and not is_last
                inner_front = front and not is_second
                f, r, e, t = i + 1, i - 1, i + 2, i - 2
                pf = 1 - pc
                if after_second:
                    first_stats(e)
                if is_second:
                    unmasked_flag(f, den_ps[:, :])
                if is_first:
                    first_stats(e)
                if inner_front:
                    z_low(f, 0)
                if is_first:
                    first_norm(e)
                    add_key_bias(0)
                    split_weights()
                    z_low(0, 0)
                if tail:
                    second_stats(t)
                if is_third:
                    prepare_scales()
                if front:
                    z_low(f, 1)
                if is_third:
                    prepare_ffn()
                if rear:
                    reciprocals(r, rear_ps[:, :])
                if is_second:
                    first_stats(e)
                    split_keys()
                if is_first:
                    add_key_bias(1)
                if tail:
                    second_norm(t)
                if front:
                    q_float(f, 0)
                if after_second:
                    first_norm(e)
                if front:
                    q_float(f, 1)
                if tail:
                    add_bias(t, 0)
                if is_second:
                    first_norm(e)
                if tail:
                    add_bias(t, 1)
                if rear:
                    attend(r, pf, 0, rear_ps[:, :])
                    attend(r, pf, 1, rear_ps[:, :])
                if is_last:
                    reciprocals(B - 1, last_den)
                if front:
                    row_max(f, 0)
                    row_max(f, 1)
                    row_max(f, 2)
                if rear:
                    residual(r, 0, rear_ps[:, :])
                if front:
                    row_max(f, 3)
                if later:
                    unmasked_flag(e, front_ps[:, :])
                if front:
                    split_max(f)
                if inner_rear:
                    residual(r, 1, rear_ps[:, :])

            all_iterations(dve, iteration)

            last_attend(0)
            last_att_low(0)
            last_attend(1)
            residual(B - 2, 1, rear_ps[:, :])
            last_att_low(1)
            second_stats(B - 2)
            last_residual(0)
            second_norm(B - 2)
            last_norm_stats(0)
            last_residual(1)
            last_norm_stats(1)
            last_second_norm(0)
            add_bias(B - 2, 0)
            last_second_norm(1)
            add_bias(B - 2, 1)
            last_add_bias(0)
            last_output(0)
            last_add_bias(1)
            last_output(1)

        @block.tensor
        def _(pe):
            mm = nc.tensor.matmul

            def project_keys(m):
                if m == 0:
                    pe.wait_ge(wq_loaded, 16)
                    pe.wait_ge(ctx_loaded, 16)
                for k in range(HALVES):
                    ins = mm(score[0][:, m * S:(m + 1) * S], wq[:, k, m * P:(m + 1) * P], ctxT[:, k], start=(k == 0),
                             stop=(k == HALVES - 1))
                ins.then_inc(kt_done, 1)

            def count_masked(e, p, bank):
                wait(pe, mt_ready, e + 1)
                if isinstance(e, int) and e == 0:
                    pe.wait_ge(c_loaded, 16 * C_LOADS)
                wait(pe, vblk_ready, e)
                mm(bank, ones_b[0:KEYS], shift[p][0:KEYS], start=True, stop=True).then_inc(masked_counted, 1)

            def z_transpose(f, m):
                wait(pe, z_ready, f + 1)
                if isinstance(f, int) and f == 0 and m == 0:
                    pe.wait_ge(c_loaded, 16 * C_LOADS)
                if m == 1:
                    wait(pe, zlo_ready, 2 * f + 1)
                elif not (isinstance(f, int) and f == 0):
                    wait(pe, flag_ready, f + 1)
                for t in range(TILES):
                    ins = nc.tensor.transpose(front_ps[:, t * P:(t + 1) * P], z[:, t, m * P:(m + 1) * P], ident)
                ins.then_inc(zt_done, 1)

            def q_project(f, m):
                wait(pe, zlo_ready, 2 * f + 2)
                if m == 1:
                    wait(pe, qf_ready, 2 * f + 1)
                if isinstance(f, int) and f == 0 and m == 0:
                    pe.wait_ge(wqlo_ready, 1)
                steps = [(a, b, k) for k in range(HALVES) for a, b in ((wq_hi, z_hi), (wq_lo, z_hi), (wq_hi, z_lo))]
                for n, (a, b, k) in enumerate(steps):
                    ins = mm(front_ps[:, :], a[:, k, m * P:(m + 1) * P], b[:, k], start=(n == 0),
                             stop=(n == len(steps) - 1))
                ins.then_inc(q_done, 1)

            def v_transpose(f):
                wait(pe, kv_ready, f + 1)
                wait(pe, qf_ready, 2 * f + 2)
                for m in range(HALVES):
                    ins = nc.tensor.transpose(front_ps[:, m * P:(m + 1) * P],
                                              kT_twice[:, m].rearrange("p a j -> p (a j)"), ident)
                ins.then_inc(v_done, 1)

            def scores_by_query(f, p, t):
                wait(pe, qhi_ready, 2 * f + 2)
                wait(pe, khi_ready, f + 1)
                wait(pe, mb_ready, f + 1)
                if t < 2:
                    wait(pe, exp_done, 4 * f - 1 + t)
                    if isinstance(f, int) and f == 0 and t == 0:
                        wait(pe, kt_ready, 2)
                else:
                    wait(pe, max_done, 4 * f + t - 1)
                for m in range(HALVES):
                    dst = score[t % 2][:, m * S:(m + 1) * S]
                    mm(dst, q_hi[:, m, t * P:(t + 1) * P], k_hi[:, m].rearrange("p h j -> p (h j)"), start=True,
                       stop=False)
                    ins = mm(dst, ident_b, mbias[:, t].unsqueeze(1).broadcast_to((P, HPH, KEYS)), start=False, stop=True)
                ins.then_inc(a_done, 1)

            def negmax_transpose(f):
                wait(pe, nm_ready, f + 1)
                if isinstance(f, int) and f == 0:
                    wait(pe, flag_ready, 1)
                wait(pe, den_copied, f)
                for t in range(TILES):
                    ins = nc.tensor.transpose(den_b[KEYS:SHIFT_ROWS, t * P:(t + 1) * P],
                                              negmax_b[:, t].rearrange("p a h -> p (a h)"), ident_b)
                ins.then_inc(nmt_done, 1)

            def scores_by_key(c, p, g):
                wait(pe, q_staged, STAGED * (c + 1))
                wait(pe, kpairs_ready, c + 1)
                wait(pe, shift_ready, c + 1)
                if g < 2:
                    wait(pe, max_done, 4 * c + g + 3)
                else:
                    wait(pe, exp_done, 4 * c + g - 1)
                for n in range(2):
                    pair = 2 * g + n
                    m, j = divmod(pair, 4)
                    dst = score[g % 2][:, n * S:(n + 1) * S]
                    mm(dst, k_pairs[p][:, pair].rearrange("p h j -> p (h j)"), q_stack[:, m, j], start=True, stop=False)
                    ins = mm(dst, shift_w[0:SHIFT_ROWS, pair], shift[p][:], start=False, stop=True)
                ins.then_inc(b_done, 1)

            def weigh_values(c, p, g):
                wait(pe, exp_done, 4 * c + g + 1)
                wait(pe, vblk_ready, c + 1)
                if g == 0:
                    wait(pe, shift_ready, c + 1)
                if g % 2 == 0:
                    wait(pe, pv_copied, 2 * c + g // 2)
                for n in range(2):
                    pair = 2 * g + n
                    m, j = divmod(pair, 4)
                    mm(pv_ps[32 * j:32 * j + 32, :], v_blk[p][:, 32 * pair:32 * pair + 32], probs[:, pair], start=True,
                       stop=True)
                for n in range(2):
                    pair = 2 * g + n
                    m, j = divmod(pair, 4)
                    jd = (j + 2) % 4
                    ins = mm(den_ps[32 * jd:32 * jd + 32, :], den_w[:, m], probs[:, pair], start=(m == 0), stop=(m == 1))
                ins.then_inc(pv_done, 1)

            def den_transpose(r):
                wait(pe, den_copied, r + 1)
                wait(pe, x1_ready, 2 * r)
                for t in range(TILES):
                    ins = nc.tensor.transpose(rear_ps[:, t * P:(t + 1) * P], den[:, t * P:(t + 1) * P], ident)
                ins.then_inc(dent_done, 1)

            def last_den_transpose():
                pe.wait_ge(den_copied, B)
                pe.wait_ge(vblk_ready, B)
                for t in range(TILES):
                    ins = nc.tensor.transpose(last_den[:, t * P:(t + 1) * P], den[:, t * P:(t + 1) * P], ident)
                ins.then_inc(dent_done, 1)

            def rden_transpose(r, m):
                wait(pe, rdenx_ready, r + 1)
                if m == 0:
                    wait(pe, y_ready, 2 * r)
                if m == 1:
                    wait(pe, att_ready, 2 * r + 1)
                for t in range(TILES):
                    ins = nc.tensor.transpose(rear_ps[:, t * P:(t + 1) * P], rden_x[:, t, m], ident)
                ins.then_inc(rdent_done, 1)

            def out_project(r, h):
                wait(pe, attlo_ready, 2 * r + 2)
                if isinstance(r, int) and r == 0 and h == 0:
                    pe.wait_ge(wolo_ready, 1)
                if h == 1:
                    wait(pe, x1_ready, 2 * r + 1)
                for t in (2 * h, 2 * h + 1):
                    dst = rear_ps[:, (t % 2) * D:(t % 2 + 1) * D]
                    steps = [(a, w, m) for m in range(HALVES)
                             for a, w in ((att_hi, wo_hi), (att_lo, wo_hi), (att_hi, wo_lo))]
                    for n, (a, w, m) in enumerate(steps):
                        ins = mm(dst, a[:, m, t * P:(t + 1) * P], w[:, m], start=(n == 0), stop=(n == len(steps) - 1))
                ins.then_inc(wo_done, 1)

            def u_transpose(r, rear):
                wait(pe, u_ready, r + 1)
                if rear:
                    wait(pe, rden_ready, r + 2)
                else:
                    wait(pe, x1_ready, 2 * r + 2)
                for m in range(HALVES):
                    for t in range(TILES):
                        ins = nc.tensor.transpose(rear_b[:, m * S + t * P:m * S + (t + 1) * P],
                                                  u[:, t, m * P:(m + 1) * P], ident_b)
                ins.then_inc(ut_done, 1)

            def ffn(r, h):
                if h == 0:
                    wait_all(pe, (wfq_ready, 1), (u8_ready, r + 1))
                else:
                    wait_all(pe, (wfq_ready, 1), (y_ready, 2 * r + 1))
                for t in (2 * h, 2 * h + 1):
                    for m in range(HALVES):
                        ins = mm(rear_ps[:, (t % 2) * D:(t % 2 + 1) * D], u8[:, m, t * P:(t + 1) * P], wf_q[:, m],
                                 start=(m == 0), stop=(m == HALVES - 1))
                ins.then_inc(y_done, 1)

            def last_rden_transpose(m):
                pe.wait_ge(rdenx_ready, B)
                pe.wait_ge(exp_done, 4 * B - 1)
                for n in range(TILES):
                    ins = nc.tensor.transpose(last_rden[m][:, n * P:(n + 1) * P], rden_x[:, n, m], ident)
                ins.then_inc(last_rdent_done, 1)

            def last_out_project(h):
                pe.wait_ge(last_attlo_ready, 2)
                pe.wait_ge(exp_done, 4 * B)
                for n in (2 * h, 2 * h + 1):
                    steps = [(a, w, m) for m in range(HALVES) for a, w in
                             ((last_att_hi, wo_hi), (last_att_lo, wo_hi), (last_att_hi, wo_lo))]
                    for k, (a, w, m) in enumerate(steps):
                        ins = mm(last_wo[h][:, (n % 2) * D:(n % 2 + 1) * D], a[:, m, n * P:(n + 1) * P], w[:, m],
                                 start=(k == 0), stop=(k == len(steps) - 1))
                ins.then_inc(last_wo_done, 1)

            def last_u_transpose(h):
                pe.wait_ge(last_u_ready, h + 1)
                if h == 0:
                    pe.wait_ge(pv_copied, 2 * B)
                else:
                    pe.wait_ge(y_ready, 2 * B - 2)
                for m in range(HALVES):
                    for n in (2 * h, 2 * h + 1):
                        ins = nc.tensor.transpose(last_ut[h][:, m * S + n * P:m * S + (n + 1) * P],
                                                  last_u[:, n, m * P:(m + 1) * P], ident_b)
                ins.then_inc(last_ut_done, 1)

            def last_ffn_project(h):
                pe.wait_ge(last_u8_ready, h + 1)
                pe.wait_ge(rden_ready, B)
                for n in (2 * h, 2 * h + 1):
                    for m in range(HALVES):
                        ins = mm(last_ffn[h][:, (n % 2) * D:(n % 2 + 1) * D], last_u8[:, m, n * P:(n + 1) * P],
                                 wf_q[:, m], start=(m == 0), stop=(m == HALVES - 1))
                ins.then_inc(last_ffn_done, 1)

            def iteration(i, pc, ahead, front, current, rear, tail):
                is_first = isinstance(i, int) and i == -2
                is_second = isinstance(i, int) and i == -1
                later = ahead and not is_first
                is_last = isinstance(i, int) and i == B - 1
                inner_rear = rear and not is_last
                inner_front = front and not is_second
                c, f, r, e, t = i, i + 1, i - 1, i + 2, i - 2
                pf = 1 - pc
                if is_first:
                    project_keys(0)
                if inner_front:
                    z_transpose(f, 0)
                if rear:
                    den_transpose(r)
                if current:
                    scores_by_key(c, pc, 0)
                if is_first:
                    z_transpose(0, 0)
                if current:
                    scores_by_key(c, pc, 1)
                if front:
                    z_transpose(f, 1)
                if current:
                    scores_by_key(c, pc, 2)
                    scores_by_key(c, pc, 3)
                if is_first:
                    project_keys(1)
                if current:
                    weigh_values(c, pc, 0)
                if front:
                    q_project(f, 0)
                if tail:
                    u_transpose(t, rear)
                if current:
                    weigh_values(c, pc, 1)
                if tail:
                    ffn(t, 0)
                if front:
                    q_project(f, 1)
                if tail:
                    ffn(t, 1)
                if current:
                    weigh_values(c, pc, 2)
                if rear:
                    rden_transpose(r, 0)
                if front:
                    v_transpose(f)
                if current:
                    weigh_values(c, pc, 3)
                if rear:
                    rden_transpose(r, 1)
                if front:
                    scores_by_query(f, pf, 0)
                    scores_by_query(f, pf, 1)
                    scores_by_query(f, pf, 2)
                if later:
                    count_masked(e, pc, front_ps[:, :])
                if is_last:
                    last_den_transpose()
                if rear:
                    out_project(r, 0)
                if front:
                    scores_by_query(f, pf, 3)
                if inner_rear:
                    out_project(r, 1)
                if front:
                    negmax_transpose(f)
                if is_first:
                    count_masked(e, pc, den_ps[:, :])

            all_iterations(pe, iteration)

            last_rden_transpose(0)
            last_rden_transpose(1)
            out_project(B - 2, 1)
            last_out_project(0)
            last_out_project(1)
            u_transpose(B - 2, False)
            ffn(B - 2, 0)
            ffn(B - 2, 1)
            last_u_transpose(0)
            last_u_transpose(1)
            last_ffn_project(0)
            last_ffn_project(1)


_INS = ["x", "mask", "mask_t", "ctx_t", "wq_t", "bq_col", "wo_t", "bo_row", "gates", "w_ffn", "s_in",
        "s_k", "bias_row", "const_f32", "const_b16"]


def kernel(**inputs):
    import numpy as _np
    import concourse.bacc as _bacc
    from concourse import mybir as _mybir
    from concourse.bass_utils import run_bass_kernel_spmd as _run

    given = {k: _np.asarray(v) for k, v in inputs.items()}
    x, keys = given["x"], given["ctx_1024"]
    batch, seq, dim = x.shape
    n_keys = keys.shape[1]
    mask = given["mask_Bx1xSxS2_if1"].reshape(batch, seq, n_keys)
    f32, b16 = constants(dim, 16, n_keys)
    keys_t = keys.transpose(0, 2, 1)
    laid = {
        "x": x,
        "mask": mask,
        "mask_t": mask.transpose(0, 2, 1),
        "ctx_t": keys_t.transpose(1, 0, 2).reshape(dim, batch * n_keys),
        "wq_t": given["L0_xattn_Wq"].T,
        "bq_col": given["L0_xattn_bq"].reshape(dim // 128, 128).T,
        "wo_t": given["L0_xattn_Wo"].T,
        "bo_row": given["L0_xattn_bo"].reshape(1, dim),
        "gates": _np.concatenate([given["g_xattn"], given["g_ffn"]]).reshape(1, 2),
        "w_ffn": given["L0_ffn_kernel"],
        "s_in": given["L0_ffn_input_scale"].reshape(1, 1),
        "s_k": given["L0_ffn_kernel_scale"].reshape(1, 1),
        "bias_row": given["L0_ffn_bias"].reshape(1, dim),
        "const_f32": f32,
        "const_b16": b16.astype(given["L0_ffn_bias"].dtype),
    }
    nc = _bacc.Bacc("TRN2", target_bir_lowering=False, num_devices=1)
    arrays, args = {}, []
    for name in _INS:
        a = _np.ascontiguousarray(laid[name])
        arrays[f"in_{name}_dram"] = a
        args.append(nc.dram_tensor(f"in_{name}_dram", a.shape, _mybir.dt.from_np(a.dtype), kind="ExternalInput").ap())
    args.append(nc.dram_tensor("out_0_dram", x.shape, _mybir.dt.from_np(x.dtype), kind="ExternalOutput").ap())
    build(nc, *args)
    return _run(nc, [arrays], core_ids=[0]).results[0]["out_0_dram"]
```
